# Optimizing a Trainium2 kernel written in Bass

```python
import numpy as np
import jax
import jax.numpy as jnp

def _softmax(x, axis=-1):
    return jax.nn.softmax(x, axis=axis)

def _gelu(x):
    return jax.nn.gelu(x, approximate=True)

def _silu(x):
    return jax.nn.silu(x)

def _sigmoid(x):
    return jax.nn.sigmoid(x)

def _layernorm(x, axis=-1, eps=1e-05):
    m = jnp.mean(x, axis=axis, keepdims=True)
    v = jnp.var(x, axis=axis, keepdims=True)
    return (x - m) / jnp.sqrt(v + eps)

def _scatter_add(tgt, idx, src, axis=0):
    return tgt.at[idx].add(src)

def _segment_sum(src, seg, n):
    return jax.ops.segment_sum(src, seg, n)
kernel_name = 'mk_decoder_preln_d2_seqx_r8_300c8e'

def setup_inputs(seed: int=0):
    np.random.seed(seed)
    _w = jnp.asarray

    def _rec_inputs():
        import jax
        import jax.numpy as jnp
        _rk = jax.random.key(seed)
        x = -0.0003929 + 0.9999 * jax.random.normal(jax.random.fold_in(_rk, 1), (4, 512, 128), jnp.float32)
        _lenS = 512 - jax.random.randint(jax.random.fold_in(_rk, 7), (4,), 0, max(1, 512 // 4) + 1, jnp.int32)
        _lenS2 = 32 - jax.random.randint(jax.random.fold_in(_rk, 8), (4,), 0, max(1, 32 // 4) + 1, jnp.int32)
        _ctx_1024P = jax.random.normal(jax.random.fold_in(_rk, 11), (4, 16, 128), jnp.float32)
        _ctx_1024c = jax.random.dirichlet(jax.random.fold_in(_rk, 511), 0.3 * jnp.ones((16,), jnp.float32), (4, 32))
        _ctx_1024t = jnp.einsum('bsk,bkd->bsd', _ctx_1024c, _ctx_1024P)
        _ctx_1024t = _ctx_1024t * jax.lax.rsqrt(jnp.mean(jnp.square(_ctx_1024t)) + 1e-12) * 0.953939
        ctx_1024 = 2.81802e-05 + 1.00001 * (_ctx_1024t + 0.3 * jax.random.normal(jax.random.fold_in(_rk, 611), (4, 32, 128), jnp.float32))
        return (x, ctx_1024)
    x, ctx_1024 = _rec_inputs()

    def _L0_attn_setup():
        import jax, jax.numpy as jnp
        import numpy as np
        B, T, D, H = (4, 128, 128, 16)
        DH = D // H
        EPS = 1e-05

        def _rwkv6(x, W_r, W_k, W_v, W_w, W_o, u, tm_r, tm_k, tm_v, tm_w, ln_w, ln_b):
            b, t, d = x.shape
            x_prev = jnp.concatenate([jnp.zeros_like(x[:, :1]), x[:, :-1]], axis=1)
            xr = tm_r * x + (1.0 - tm_r) * x_prev
            xk = tm_k * x + (1.0 - tm_k) * x_prev
            xv = tm_v * x + (1.0 - tm_v) * x_prev
            xw = tm_w * x + (1.0 - tm_w) * x_prev
            r = jax.nn.sigmoid(xr @ W_r.T)
            k = xk @ W_k.T
            v = xv @ W_v.T
            w = -jax.nn.softplus(-(xw @ W_w.T)) - 0.0001
            r = r.reshape(b, t, H, DH)
            k = k.reshape(b, t, H, DH)
            v = v.reshape(b, t, H, DH)
            w = w.reshape(b, t, H, DH)

            def step(s, rkvw):
                r_t, k_t, v_t, w_t = rkvw
                bonus = jnp.exp(u + k_t)[..., :, None] * v_t[..., None, :]
                o_t = jnp.einsum('bhi,bhij->bhj', r_t, s + bonus)
                s = jnp.exp(w_t)[..., None] * s + k_t[..., :, None] * v_t[..., None, :]
                return (s, o_t)
            s0 = jnp.zeros((b, H, DH, DH), x.dtype)
            rkvw = tuple((a.transpose(1, 0, 2, 3) for a in (r, k, v, w)))
            _, o = jax.lax.scan(step, s0, rkvw)
            o = o.transpose(1, 0, 2, 3)
            mu = jnp.mean(o, axis=-1, keepdims=True)
            var = jnp.var(o, axis=-1, keepdims=True)
            o = (o - mu) * jax.lax.rsqrt(var + EPS) * ln_w + ln_b
            o = o * r
            return o.reshape(b, t, d) @ W_o.T
        key = jax.random.key(seed)
        ks = jax.random.split(key, 14)
        sc = 1.0 / np.sqrt(D)
        x = jax.random.normal(ks[0], (B, T, D), jnp.float32)
        W_r = jax.random.normal(ks[1], (D, D), jnp.float32) * sc
        W_k = jax.random.normal(ks[2], (D, D), jnp.float32) * sc
        W_v = jax.random.normal(ks[3], (D, D), jnp.float32) * sc
        W_w = jax.random.normal(ks[4], (D, D), jnp.float32) * sc
        W_o = jax.random.normal(ks[5], (D, D), jnp.float32) * sc
        u = jax.random.normal(ks[6], (H, DH), jnp.float32) * 0.1
        tm_r = jax.random.uniform(ks[7], (D,), jnp.float32)
        tm_k = jax.random.uniform(ks[8], (D,), jnp.float32)
        tm_v = jax.random.uniform(ks[9], (D,), jnp.float32)
        tm_w = jax.random.uniform(ks[10], (D,), jnp.float32)
        ln_w = jnp.ones((DH,), jnp.float32) + 0.1 * jax.random.normal(ks[11], (DH,), jnp.float32)
        ln_b = 0.1 * jax.random.normal(ks[12], (DH,), jnp.float32)
        return {'x': x, 'W_r': W_r, 'W_k': W_k, 'W_v': W_v, 'W_w': W_w, 'W_o': W_o, 'u': u, 'tm_r': tm_r, 'tm_k': tm_k, 'tm_v': tm_v, 'tm_w': tm_w, 'ln_w': ln_w, 'ln_b': ln_b}
    _L0_attn_all = _L0_attn_setup()
    _L0_attn_in = {k: v for k, v in _L0_attn_all.items() if k in ('W_r', 'W_k', 'W_v', 'W_w', 'W_o', 'u', 'tm_r', 'tm_k', 'tm_v', 'tm_w', 'ln_w', 'ln_b')}
    del _L0_attn_all

    def _L0_xattn_setup():
        import jax, jax.numpy as jnp
        import numpy as np
        B, LQ, LKV, D = (8, 256, 256, 128)
        key = jax.random.key(seed)
        k1, k2, k3, k4, k5, k6, k7 = jax.random.split(key, 7)
        s = 1.0 / np.sqrt(D)
        return {'query': jax.random.normal(k1, (B, LQ, D), jnp.float32), 'key': jax.random.normal(k2, (B, LKV, D), jnp.float32), 'value': jax.random.normal(k3, (B, LKV, D), jnp.float32), 'Wq': jax.random.uniform(k4, (D, D), jnp.float32, -s, s), 'bq': jax.random.uniform(k5, (D,), jnp.float32, -s, s), 'Wk': jax.random.uniform(k6, (D, D), jnp.float32, -s, s), 'bk': jax.random.uniform(k7, (D,), jnp.float32, -s, s), 'scale_factor': 32, 'dropout_p': 0}
    _L0_xattn_all = _L0_xattn_setup()
    _L0_xattn_in = {k: v for k, v in _L0_xattn_all.items() if k in ('Wq', 'bq', 'Wk', 'bk')}
    del _L0_xattn_all

    def _L0_ffn_setup():
        import jax, jax.numpy as jnp
        import numpy as np
        D = 128
        H = 16
        FF = 512
        E = 8
        K = 2
        EH = 128
        B, S = (2, 256)
        EPS = 1e-05

        def rmsnorm(x, w):
            v = jnp.mean(jnp.square(x), axis=-1, keepdims=True)
            return x * jax.lax.rsqrt(v + EPS) * w

        def _dense_path(x, wq, wk, wv, wo, w1, w2, w3, attn_norm_w, ff_norm_w):
            b, s, d = x.shape
            hd = d // H
            q = (x @ wq).reshape(b, s, H, hd)
            k = (x @ wk).reshape(b, s, H, hd)
            v = (x @ wv).reshape(b, s, H, hd)
            scores = jnp.einsum('bqhd,bkhd->bhqk', q, k) / np.sqrt(hd).astype(np.float32)
            causal = jnp.tril(jnp.ones((s, s), bool))
            scores = jnp.where(causal, scores, jnp.finfo(scores.dtype).min)
            attn = jax.nn.softmax(scores, axis=-1)
            o = jnp.einsum('bhqk,bkhd->bqhd', attn, v).reshape(b, s, d)
            h = x + rmsnorm(o @ wo, attn_norm_w)
            ffn = jax.nn.silu(h @ w1) * (h @ w3) @ w2
            return h + rmsnorm(ffn, ff_norm_w)

        def _sparse_path(x, router_w, ew1, ew2, ew3, moe_norm_w):
            b, s, d = x.shape
            xt = x.reshape(-1, d)
            probs = jax.nn.softmax(xt @ router_w, axis=-1)
            topw, topi = jax.lax.top_k(probs, K)
            g = jax.nn.silu(jnp.einsum('td,edh->eth', xt, ew1)) * jnp.einsum('td,edh->eth', xt, ew3)
            eo = jnp.einsum('eth,ehd->ted', g, ew2)
            sel = jnp.take_along_axis(eo, topi[:, :, None], axis=1)
            moe_out = jnp.sum(topw[:, :, None] * sel, axis=1).reshape(b, s, d)
            return rmsnorm(moe_out, moe_norm_w)
        key = jax.random.key(seed)
        ks = jax.random.split(key, 16)
        s = 0.02
        return {'x': jax.random.normal(ks[0], (B, S, D), jnp.float32), 'wq': jax.random.normal(ks[1], (D, D), jnp.float32) * s, 'wk': jax.random.normal(ks[2], (D, D), jnp.float32) * s, 'wv': jax.random.normal(ks[3], (D, D), jnp.float32) * s, 'wo': jax.random.normal(ks[4], (D, D), jnp.float32) * s, 'w1': jax.random.normal(ks[5], (D, FF), jnp.float32) * s, 'w2': jax.random.normal(ks[6], (FF, D), jnp.float32) * s, 'w3': jax.random.normal(ks[7], (D, FF), jnp.float32) * s, 'attn_norm_w': jnp.ones((D,), jnp.float32), 'ff_norm_w': jnp.ones((D,), jnp.float32), 'moe_norm_w': jnp.ones((D,), jnp.float32), 'router_w': jax.random.normal(ks[8], (D, E), jnp.float32) * s, 'ew1': jax.random.normal(ks[9], (E, D, EH), jnp.float32) * s, 'ew2': jax.random.normal(ks[10], (E, EH, D), jnp.float32) * s, 'ew3': jax.random.normal(ks[11], (E, D, EH), jnp.float32) * s}
    _L0_ffn_all = _L0_ffn_setup()
    _L0_ffn_in = {k: v for k, v in _L0_ffn_all.items() if k in ('wq', 'wk', 'wv', 'wo', 'w1', 'w2', 'w3', 'attn_norm_w', 'ff_norm_w', 'moe_norm_w', 'router_w', 'ew1', 'ew2', 'ew3')}
    del _L0_ffn_all

    def _L1_attn_setup():
        import jax, jax.numpy as jnp
        import numpy as np
        B, S, D, H, R = (2, 256, 128, 16, 64)
        HD = D // H
        VOCAB = 2 * R + 1
        key = jax.random.key(seed)
        ks = jax.random.split(key, 7)
        s = 0.02
        return {'x': jax.random.normal(ks[0], (B, S, D), jnp.float32), 'W_qkv': jax.random.normal(ks[1], (D, 3 * D), jnp.float32) * s, 'b_qkv': jnp.zeros((3 * D,), jnp.float32), 'W_out': jax.random.normal(ks[2], (D, D), jnp.float32) * s, 'b_out': jnp.zeros((D,), jnp.float32), 'rel_emb_k': jax.random.normal(ks[3], (VOCAB, HD), jnp.float32) * s, 'rel_emb_v': jax.random.normal(ks[4], (VOCAB, HD), jnp.float32) * s}
    _L1_attn_all = _L1_attn_setup()
    _L1_attn_in = {k: v for k, v in _L1_attn_all.items() if k in ('W_qkv', 'b_qkv', 'W_out', 'b_out', 'rel_emb_k', 'rel_emb_v')}
    del _L1_attn_all

    def _L1_xattn_setup():
        import jax, jax.numpy as jnp
        import numpy as np
        DIM = 128
        H = 16
        D = 64
        INNER = H * D
        EPS = 1e-05

        def layernorm(x, w, b):
            mu = jnp.mean(x, axis=-1, keepdims=True)
            var = jnp.var(x, axis=-1, keepdims=True)
            return (x - mu) * jax.lax.rsqrt(var + EPS) * w + b
        key = jax.random.key(seed)
        ks = jax.random.split(key, 8)
        B, N, S = (4, 32, 1024)
        s = 1.0 / np.sqrt(DIM)
        return {'latents': jax.random.normal(ks[0], (B, N, DIM), jnp.float32), 'context': jax.random.normal(ks[1], (B, S, DIM), jnp.float32), 'ln_l_w': jnp.ones((DIM,), jnp.float32), 'ln_l_b': jnp.zeros((DIM,), jnp.float32), 'ln_c_w': jnp.ones((DIM,), jnp.float32), 'ln_c_b': jnp.zeros((DIM,), jnp.float32), 'Wq': jax.random.normal(ks[2], (DIM, INNER), jnp.float32) * s, 'Wkv': jax.random.normal(ks[3], (DIM, 2 * INNER), jnp.float32) * s, 'Wo': jax.random.normal(ks[4], (INNER, DIM), jnp.float32) * (1.0 / np.sqrt(INNER)), 'bo': jnp.zeros((DIM,), jnp.float32)}
    _L1_xattn_all = _L1_xattn_setup()
    _L1_xattn_in = {k: v for k, v in _L1_xattn_all.items() if k in ('ln_l_w', 'ln_l_b', 'ln_c_w', 'ln_c_b', 'Wq', 'Wkv', 'Wo', 'bo')}
    del _L1_xattn_all

    def _L1_ffn_setup():
        import jax, jax.numpy as jnp
        import numpy as np
        B, N, C, H, REG = (1, 2309, 128, 16, 5)
        D = C // H
        key = jax.random.key(seed)
        k0, k1, k2, k3 = jax.random.split(key, 4)
        x = jax.random.normal(k0, (B, N, C), dtype=jnp.float32)
        g_info = jax.random.normal(k1, (12, 2, C), dtype=jnp.float32)
        W_qkv = jax.random.normal(k2, (C, 3 * C), dtype=jnp.float32) * 0.02
        W_proj = jax.random.normal(k3, (C, C), dtype=jnp.float32) * 0.02
        b_proj = jnp.zeros((C,), dtype=jnp.float32)
        return {'x': x, 'g_info': g_info, 'W_qkv': W_qkv, 'W_proj': W_proj, 'b_proj': b_proj}
    _L1_ffn_all = _L1_ffn_setup()
    _L1_ffn_in = {k: v for k, v in _L1_ffn_all.items() if k in ('g_info', 'W_qkv', 'W_proj', 'b_proj')}
    del _L1_ffn_all
    return {'x': x, 'ctx_1024': ctx_1024, 'L0_attn_W_r': _L0_attn_in['W_r'], 'L0_attn_W_k': _L0_attn_in['W_k'], 'L0_attn_W_v': _L0_attn_in['W_v'], 'L0_attn_W_w': _L0_attn_in['W_w'], 'L0_attn_W_o': _L0_attn_in['W_o'], 'L0_attn_u': _L0_attn_in['u'], 'L0_attn_tm_r': _L0_attn_in['tm_r'], 'L0_attn_tm_k': _L0_attn_in['tm_k'], 'L0_attn_tm_v': _L0_attn_in['tm_v'], 'L0_attn_tm_w': _L0_attn_in['tm_w'], 'L0_attn_ln_w': _L0_attn_in['ln_w'], 'L0_attn_ln_b': _L0_attn_in['ln_b'], 'L0_xattn_Wq': _L0_xattn_in['Wq'], 'L0_xattn_bq': _L0_xattn_in['bq'], 'L0_xattn_Wk': _L0_xattn_in['Wk'], 'L0_xattn_bk': _L0_xattn_in['bk'], 'L0_ffn_wq': _L0_ffn_in['wq'], 'L0_ffn_wk': _L0_ffn_in['wk'], 'L0_ffn_wv': _L0_ffn_in['wv'], 'L0_ffn_wo': _L0_ffn_in['wo'], 'L0_ffn_w1': _L0_ffn_in['w1'], 'L0_ffn_w2': _L0_ffn_in['w2'], 'L0_ffn_w3': _L0_ffn_in['w3'], 'L0_ffn_attn_norm_w': _L0_ffn_in['attn_norm_w'], 'L0_ffn_ff_norm_w': _L0_ffn_in['ff_norm_w'], 'L0_ffn_moe_norm_w': _L0_ffn_in['moe_norm_w'], 'L0_ffn_router_w': _L0_ffn_in['router_w'], 'L0_ffn_ew1': _L0_ffn_in['ew1'], 'L0_ffn_ew2': _L0_ffn_in['ew2'], 'L0_ffn_ew3': _L0_ffn_in['ew3'], 'L1_attn_W_qkv': _L1_attn_in['W_qkv'], 'L1_attn_b_qkv': _L1_attn_in['b_qkv'], 'L1_attn_W_out': _L1_attn_in['W_out'], 'L1_attn_b_out': _L1_attn_in['b_out'], 'L1_attn_rel_emb_k': _L1_attn_in['rel_emb_k'], 'L1_attn_rel_emb_v': _L1_attn_in['rel_emb_v'], 'L1_xattn_ln_l_w': _L1_xattn_in['ln_l_w'], 'L1_xattn_ln_l_b': _L1_xattn_in['ln_l_b'], 'L1_xattn_ln_c_w': _L1_xattn_in['ln_c_w'], 'L1_xattn_ln_c_b': _L1_xattn_in['ln_c_b'], 'L1_xattn_Wq': _L1_xattn_in['Wq'], 'L1_xattn_Wkv': _L1_xattn_in['Wkv'], 'L1_xattn_Wo': _L1_xattn_in['Wo'], 'L1_xattn_bo': _L1_xattn_in['bo'], 'L1_ffn_g_info': _L1_ffn_in['g_info'], 'L1_ffn_W_qkv': _L1_ffn_in['W_qkv'], 'L1_ffn_W_proj': _L1_ffn_in['W_proj'], 'L1_ffn_b_proj': _L1_ffn_in['b_proj']}

def reference(x, ctx_1024, L0_attn_W_r, L0_attn_W_k, L0_attn_W_v, L0_attn_W_w, L0_attn_W_o, L0_attn_u, L0_attn_tm_r, L0_attn_tm_k, L0_attn_tm_v, L0_attn_tm_w, L0_attn_ln_w, L0_attn_ln_b, L0_xattn_Wq, L0_xattn_bq, L0_xattn_Wk, L0_xattn_bk, L0_ffn_wq, L0_ffn_wk, L0_ffn_wv, L0_ffn_wo, L0_ffn_w1, L0_ffn_w2, L0_ffn_w3, L0_ffn_attn_norm_w, L0_ffn_ff_norm_w, L0_ffn_moe_norm_w, L0_ffn_router_w, L0_ffn_ew1, L0_ffn_ew2, L0_ffn_ew3, L1_attn_W_qkv, L1_attn_b_qkv, L1_attn_W_out, L1_attn_b_out, L1_attn_rel_emb_k, L1_attn_rel_emb_v, L1_xattn_ln_l_w, L1_xattn_ln_l_b, L1_xattn_ln_c_w, L1_xattn_ln_c_b, L1_xattn_Wq, L1_xattn_Wkv, L1_xattn_Wo, L1_xattn_bo, L1_ffn_g_info, L1_ffn_W_qkv, L1_ffn_W_proj, L1_ffn_b_proj):
    import jax
    import jax.numpy as jnp

    def _L0_attn_ref(x, W_r, W_k, W_v, W_w, W_o, u, tm_r, tm_k, tm_v, tm_w, ln_w, ln_b):
        import jax, jax.numpy as jnp
        import numpy as np
        B, T, D, H = (4, 128, 128, 16)
        DH = D // H
        EPS = 1e-05

        def _rwkv6(x, W_r, W_k, W_v, W_w, W_o, u, tm_r, tm_k, tm_v, tm_w, ln_w, ln_b):
            b, t, d = x.shape
            x_prev = jnp.concatenate([jnp.zeros_like(x[:, :1]), x[:, :-1]], axis=1)
            xr = tm_r * x + (1.0 - tm_r) * x_prev
            xk = tm_k * x + (1.0 - tm_k) * x_prev
            xv = tm_v * x + (1.0 - tm_v) * x_prev
            xw = tm_w * x + (1.0 - tm_w) * x_prev
            r = jax.nn.sigmoid(xr @ W_r.T)
            k = xk @ W_k.T
            v = xv @ W_v.T
            w = -jax.nn.softplus(-(xw @ W_w.T)) - 0.0001
            r = r.reshape(b, t, H, DH)
            k = k.reshape(b, t, H, DH)
            v = v.reshape(b, t, H, DH)
            w = w.reshape(b, t, H, DH)

            def step(s, rkvw):
                r_t, k_t, v_t, w_t = rkvw
                bonus = jnp.exp(u + k_t)[..., :, None] * v_t[..., None, :]
                o_t = jnp.einsum('bhi,bhij->bhj', r_t, s + bonus)
                s = jnp.exp(w_t)[..., None] * s + k_t[..., :, None] * v_t[..., None, :]
                return (s, o_t)
            s0 = jnp.zeros((b, H, DH, DH), x.dtype)
            rkvw = tuple((a.transpose(1, 0, 2, 3) for a in (r, k, v, w)))
            _, o = jax.lax.scan(step, s0, rkvw)
            o = o.transpose(1, 0, 2, 3)
            mu = jnp.mean(o, axis=-1, keepdims=True)
            var = jnp.var(o, axis=-1, keepdims=True)
            o = (o - mu) * jax.lax.rsqrt(var + EPS) * ln_w + ln_b
            o = o * r
            return o.reshape(b, t, d) @ W_o.T
        return _rwkv6(x, W_r, W_k, W_v, W_w, W_o, u, tm_r, tm_k, tm_v, tm_w, ln_w, ln_b)

    def _L0_xattn_ref(query, key, value, Wq, bq, Wk, bk, scale_factor, dropout_p):
        import jax, jax.numpy as jnp
        import numpy as np
        B, LQ, LKV, D = (8, 256, 256, 128)
        q = jnp.einsum('bld,ed->ble', query, Wq) + bq
        k = jnp.einsum('bld,ed->ble', key, Wk) + bk
        scores = jnp.einsum('bqd,bkd->bqk', q, k) / jnp.float32(scale_factor)
        attn = jax.nn.softmax(scores, axis=-1)
        return jnp.einsum('bqk,bkd->bqd', attn, value)

    def _L0_ffn_ref(x, wq, wk, wv, wo, w1, w2, w3, attn_norm_w, ff_norm_w, moe_norm_w, router_w, ew1, ew2, ew3):
        import jax, jax.numpy as jnp
        import numpy as np
        D = 128
        H = 16
        FF = 512
        E = 8
        K = 2
        EH = 128
        B, S = (2, 256)
        EPS = 1e-05

        def rmsnorm(x, w):
            v = jnp.mean(jnp.square(x), axis=-1, keepdims=True)
            return x * jax.lax.rsqrt(v + EPS) * w

        def _dense_path(x, wq, wk, wv, wo, w1, w2, w3, attn_norm_w, ff_norm_w):
            b, s, d = x.shape
            hd = d // H
            q = (x @ wq).reshape(b, s, H, hd)
            k = (x @ wk).reshape(b, s, H, hd)
            v = (x @ wv).reshape(b, s, H, hd)
            scores = jnp.einsum('bqhd,bkhd->bhqk', q, k) / np.sqrt(hd).astype(np.float32)
            causal = jnp.tril(jnp.ones((s, s), bool))
            scores = jnp.where(causal, scores, jnp.finfo(scores.dtype).min)
            attn = jax.nn.softmax(scores, axis=-1)
            o = jnp.einsum('bhqk,bkhd->bqhd', attn, v).reshape(b, s, d)
            h = x + rmsnorm(o @ wo, attn_norm_w)
            ffn = jax.nn.silu(h @ w1) * (h @ w3) @ w2
            return h + rmsnorm(ffn, ff_norm_w)

        def _sparse_path(x, router_w, ew1, ew2, ew3, moe_norm_w):
            b, s, d = x.shape
            xt = x.reshape(-1, d)
            probs = jax.nn.softmax(xt @ router_w, axis=-1)
            topw, topi = jax.lax.top_k(probs, K)
            g = jax.nn.silu(jnp.einsum('td,edh->eth', xt, ew1)) * jnp.einsum('td,edh->eth', xt, ew3)
            eo = jnp.einsum('eth,ehd->ted', g, ew2)
            sel = jnp.take_along_axis(eo, topi[:, :, None], axis=1)
            moe_out = jnp.sum(topw[:, :, None] * sel, axis=1).reshape(b, s, d)
            return rmsnorm(moe_out, moe_norm_w)
        dense_out = _dense_path(x, wq, wk, wv, wo, w1, w2, w3, attn_norm_w, ff_norm_w)
        sparse_out = _sparse_path(x, router_w, ew1, ew2, ew3, moe_norm_w)
        return dense_out + sparse_out

    def _L1_attn_ref(x, W_qkv, b_qkv, W_out, b_out, rel_emb_k, rel_emb_v):
        import jax, jax.numpy as jnp
        import numpy as np
        B, S, D, H, R = (2, 256, 128, 16, 64)
        HD = D // H
        VOCAB = 2 * R + 1
        b, s, d = x.shape
        hd = d // H
        idx = jnp.arange(s)
        dist = jnp.clip(idx[None, :] - idx[:, None], -R, R) + R
        pe_k = rel_emb_k[dist]
        pe_v = rel_emb_v[dist]
        qkv = (x @ W_qkv + b_qkv).reshape(b, s, 3, H, hd)
        qkv = jnp.transpose(qkv, (2, 0, 3, 1, 4))
        q, k, v = (qkv[0], qkv[1], qkv[2])
        q = q / jnp.sqrt(jnp.asarray(hd, x.dtype))
        score = jnp.einsum('bhqd,bhkd->bhqk', q, k) + jnp.einsum('bhqd,qkd->bhqk', q, pe_k)
        attn = jax.nn.softmax(score, axis=-1)
        ctx = jnp.einsum('bhqk,bhkd->bhqd', attn, v) + jnp.einsum('bhqk,qkd->bhqd', attn, pe_v)
        ctx = jnp.transpose(ctx, (0, 2, 1, 3)).reshape(b, s, d)
        return ctx @ W_out + b_out

    def _L1_xattn_ref(latents, context, ln_l_w, ln_l_b, ln_c_w, ln_c_b, Wq, Wkv, Wo, bo):
        import jax, jax.numpy as jnp
        import numpy as np
        DIM = 128
        H = 16
        D = 64
        INNER = H * D
        EPS = 1e-05

        def layernorm(x, w, b):
            mu = jnp.mean(x, axis=-1, keepdims=True)
            var = jnp.var(x, axis=-1, keepdims=True)
            return (x - mu) * jax.lax.rsqrt(var + EPS) * w + b
        b, n, _ = latents.shape
        s = context.shape[1]
        lat = layernorm(latents, ln_l_w, ln_l_b)
        ctx = layernorm(context, ln_c_w, ln_c_b)
        q = (lat @ Wq).reshape(b, n, H, D).transpose(0, 2, 1, 3)
        kv = ctx @ Wkv
        k, v = jnp.split(kv, 2, axis=-1)
        k = k.reshape(b, s, H, D).transpose(0, 2, 1, 3)
        v = v.reshape(b, s, H, D).transpose(0, 2, 1, 3)
        scale = D ** (-0.5)
        attn = jnp.einsum('bhnd,bhsd->bhns', q, k) * scale
        attn = jnp.clip(attn, -11.0, 11.0)
        attn = jax.nn.softmax(attn, axis=-1)
        out = jnp.einsum('bhns,bhsd->bhnd', attn, v)
        out = out.transpose(0, 2, 1, 3).reshape(b, n, INNER)
        return out @ Wo + bo

    def _L1_ffn_ref(x, g_info, W_qkv, W_proj, b_proj):
        import jax, jax.numpy as jnp
        import numpy as np
        B, N, C, H, REG = (1, 2309, 128, 16, 5)
        D = C // H
        Bx, Nx, Cx = x.shape
        scale = D ** (-0.5)
        qkv = (x @ W_qkv).reshape(Bx, Nx, 3, H, D)
        q, k, v = (qkv[:, :, 0], qkv[:, :, 1], qkv[:, :, 2])
        g_layer = g_info[0].reshape(-1, H, D)
        q_g = g_layer[0]
        q_pure = q[:, REG:]
        q_n = q_pure / jnp.linalg.norm(q_pure, axis=-1, keepdims=True)
        qg_n = q_g / jnp.linalg.norm(q_g, axis=-1, keepdims=True)
        sim = (qg_n[None, None] * q_n).sum(-1).mean(-1)
        sim = (sim - sim.min()) / (sim.max() - sim.min())
        pos = sim > 0.9
        logits = jnp.einsum('bqhd,bkhd->bhqk', q * scale, k)

        def masked_attn(tok_mask):
            key_mask = jnp.concatenate([jnp.ones((Bx, REG), bool), tok_mask], axis=1)
            l = jnp.where(key_mask[:, None, None, :], logits, -jnp.inf)
            a = jax.nn.softmax(l, axis=-1)
            return jnp.einsum('bhqk,bkhd->bqhd', a, v)
        x_pos = masked_attn(pos)
        x_neg = masked_attn(~pos)
        reg_out = (x_pos[:, :REG] + x_neg[:, :REG]) * 0.5
        tok_out = jnp.where(pos[:, :, None, None], x_pos[:, REG:], x_neg[:, REG:])
        out = jnp.concatenate([reg_out, tok_out], axis=1).reshape(Bx, Nx, Cx)
        return out @ W_proj + b_proj
    x = x + _L0_attn_ref(_layernorm(x, axis=-1), L0_attn_W_r, L0_attn_W_k, L0_attn_W_v, L0_attn_W_w, L0_attn_W_o, L0_attn_u, L0_attn_tm_r, L0_attn_tm_k, L0_attn_tm_v, L0_attn_tm_w, L0_attn_ln_w, L0_attn_ln_b)
    x = x + _L0_xattn_ref(_layernorm(x, axis=-1), ctx_1024, ctx_1024, L0_xattn_Wq, L0_xattn_bq, L0_xattn_Wk, L0_xattn_bk, 32, 0)
    x = x + _L0_ffn_ref(_layernorm(x, axis=-1), L0_ffn_wq, L0_ffn_wk, L0_ffn_wv, L0_ffn_wo, L0_ffn_w1, L0_ffn_w2, L0_ffn_w3, L0_ffn_attn_norm_w, L0_ffn_ff_norm_w, L0_ffn_moe_norm_w, L0_ffn_router_w, L0_ffn_ew1, L0_ffn_ew2, L0_ffn_ew3)
    x = x + _L1_attn_ref(_layernorm(x, axis=-1), L1_attn_W_qkv, L1_attn_b_qkv, L1_attn_W_out, L1_attn_b_out, L1_attn_rel_emb_k, L1_attn_rel_emb_v)
    x = x + _L1_xattn_ref(_layernorm(x, axis=-1), ctx_1024, L1_xattn_ln_l_w, L1_xattn_ln_l_b, L1_xattn_ln_c_w, L1_xattn_ln_c_b, L1_xattn_Wq, L1_xattn_Wkv, L1_xattn_Wo, L1_xattn_bo)
    x = x + _L1_ffn_ref(_layernorm(x, axis=-1), L1_ffn_g_info, L1_ffn_W_qkv, L1_ffn_W_proj, L1_ffn_b_proj)
    return x

_drawn_inputs = setup_inputs


def setup_inputs(seed=0):
    import zlib

    import numpy as np

    out = dict(_drawn_inputs(seed))
    spreads = {'L0_ffn_attn_norm_w': (1.0, 0.2),
     'L0_ffn_ff_norm_w': (1.0, 0.2),
     'L0_ffn_moe_norm_w': (1.0, 0.582),
     'L1_attn_b_qkv': (0.0, 0.8),
     'L1_attn_b_out': (0.0, 0.1),
     'L1_xattn_ln_l_w': (1.0, 0.6),
     'L1_xattn_ln_l_b': (0.0, 0.8),
     'L1_xattn_ln_c_w': (1.0, 0.2),
     'L1_xattn_ln_c_b': (0.0, 0.1),
     'L1_xattn_bo': (0.0, 0.1),
     'L1_ffn_b_proj': (0.0, 0.1)}
    factors = {'L0_attn_u': 6.46,
     'L0_attn_tm_w': 2.958,
     'L0_xattn_bq': 8.0,
     'L0_xattn_bk': 64.0,
     'L0_ffn_wq': 7.602,
     'L0_ffn_wk': 7.366,
     'L1_attn_W_qkv': 5.286,
     'L1_attn_W_out': 3.926,
     'L1_attn_rel_emb_k': 45.041,
     'L1_attn_rel_emb_v': 8.0,
     'L1_ffn_g_info': 28.547,
     'L1_ffn_W_qkv': 5.179,
     'L1_ffn_W_proj': 5.471}
    for name, (base, spread) in spreads.items():
        noise = np.random.default_rng([zlib.crc32(name.encode()), seed]).standard_normal(out[name].shape)
        drawn = base * np.exp(spread * noise) if base else spread * noise
        out[name] = jnp.asarray(drawn.astype(out[name].dtype))
    for name, factor in factors.items():
        out[name] = (out[name] * factor).astype(out[name].dtype)
    return out
```

```python
import concourse.bass as bass
from concourse import mybir
from contextlib import ExitStack, contextmanager
import numpy as np

B, T, D = 4, 512, 128
NT = B * T
H, HD = 16, 8
LC = 32
FF = 512
E, EH = 8, 128
XH, XD = 16, 64
REL = 64
REG = 5
BIG = 1.0e30
EPS = 1e-05
QT = T // 128

fp32 = mybir.dt.float32
bf16 = mybir.dt.bfloat16
ALU = mybir.AluOpType
ACT = mybir.ActivationFunctionType
AX = mybir.AxisListType

WEIGHT_COLS = {}
_at = 0
for _n, _w in (("r", D), ("k", D), ("w", D), ("v", D), ("vrep", HD * D), ("o", D),
               ("xq", D), ("xk", D),
               ("fq", D), ("fk", D), ("fv", D), ("fo", D), ("w1", FF), ("w3", FF), ("w2", FF),
               ("router", E), ("ew1", E * EH), ("ew3", E * EH), ("ew2", E * D),
               ("aqkv", 3 * D), ("aout", D),
               ("lq", XH * XD), ("lkv", 2 * XH * XD), ("lo", XH * XD // 128 * D),
               ("gqkv", 3 * D), ("gproj", D)):
    WEIGHT_COLS[_n] = (_at, _w)
    _at += _w
    if _n == "ew2":
        LAYER_WIDTH, _at = _at, 0
assert _at <= LAYER_WIDTH
WEIGHT_WIDTH = LAYER_WIDTH + _at
WEIGHT_GROUPS = (("r", "o"), ("xq", "xk"), ("fq", "fo"), ("w1", "router"), ("ew1", "ew2"),
                 ("aqkv", "aout"), ("lq", "lo"), ("gqkv", "gproj"))
LAYER_0_GROUPS = 5

VECTORS = ("tm_r", "tm_k", "tm_v", "tm_w", "u", "ln_w", "ln_b", "bq", "bk",
           "attn_norm_w", "ff_norm_w", "moe_norm_w", "b_q", "b_k", "b_v", "b_out",
           "ln_l_w", "ln_l_b", "ln_c_w", "ln_c_b", "bo", "g_q", "b_proj", "rel_k_lo", "rel_k_hi")
VEC = {n: i for i, n in enumerate(VECTORS)}


def shape_constants():
    ch = np.arange(D)
    head, within = ch // HD, ch % HD
    out = {}
    out["ident"] = np.eye(D)
    out["center"] = np.eye(D) - 1.0 / D
    out["mean"] = np.full((D, D), 1.0 / D)
    same = (head[:, None] == head[None, :]).astype(float)
    out["hcenter"] = np.eye(D) - same / HD
    out["hmean"] = same / HD
    out["hsum"] = same
    out["hsel"] = np.concatenate([same * (within[None, :] == j) for j in range(HD)], 1)
    ones_at = lambda pairs, m: (lambda a: ([a.__setitem__(p, 1.0) for p in pairs], a)[1])(np.zeros((D, m)))
    for grp in range(4):
        out[f"dense{grp}"] = ones_at([(32 * j + d, (4 * grp + j) * HD + d) for j in range(4) for d in range(HD)], D)
    for grp in range(4):
        out[f"sums{grp}"] = ones_at([(32 * j + HD, r * H + 4 * grp + j) for j in range(4) for r in range(2)], 32)
    out["spread"] = ones_at([(32 * b + h, h * HD + d) for b in range(4) for h in range(H) for d in range(HD)], D)
    out["lowered"] = -BIG * (ch[None, :] > ch[:, None])
    out["loweredT"] = -BIG * (ch[:, None] > ch[None, :])
    out["order"] = np.tile(E - np.arange(E), (D, 1))
    out["to_dh"] = ones_at([(h * HD + d, d * H + h) for h in range(H) for d in range(HD)], D)
    c, h = ch // H, ch % H
    out["own_c"] = (ch[:, None] // HD == c[None, :]).astype(float)
    out["own_pair"] = (1 - c[:, None] % 2 == np.arange(2 * HD)[None, :] // HD).astype(float)
    out["headmask"] = (head[:, None] == np.arange(H)[None, :]).astype(float)
    return out


CONST_COLS = {}
_at = 0
for _n, _a in shape_constants().items():
    CONST_COLS[_n] = (_at, _a.shape[1])
    _at += _a.shape[1]
CONST_WIDTH = _at


class Core:
    pass


@contextmanager
def semaphores(nc, tag):
    taken = []

    def sem(name):
        taken.append(nc.alloc_semaphore(f"{tag}_{name}"))
        return taken[-1]
    yield sem
    nc.clear_and_free_semaphores(taken)
    nc.all_engine_barrier()


def load_stage(nc, g, ins):
    with nc.Block() as block:
        @block.sync
        def _(sp):
            sp.dma_start(g.x[:, :], ins["xT"]).then_inc(g.x_loaded, 16)
            sp.dma_start(g.const[:, :], ins["const"]).then_inc(g.const_loaded, 16)
            sp.dma_start(g.ctxT[:, :], ins["ctxT"]).then_inc(g.ctx_loaded, 16)
            sp.dma_start(g.ctx[:, :, :], ins["ctx"]).then_inc(g.ctx_loaded, 16)
            sp.dma_start(g.vec[:, :], ins["vec"]).then_inc(g.vec_loaded, 16)
            for n, (first, last) in enumerate(WEIGHT_GROUPS[:LAYER_0_GROUPS]):
                a, z = WEIGHT_COLS[first][0], sum(WEIGHT_COLS[last])
                sp.dma_start(g.weights[:, a:z], ins["weights"][:, a:z]).then_inc(g.weights_loaded[n], 16)


def load_layer_1(nc, g, ins):
    with nc.Block() as block:
        @block.sync
        def _(sp):
            for n in range(LAYER_0_GROUPS):
                sp.wait_ge(g.weights_loaded[n], 16)
            for n, (first, last) in list(enumerate(WEIGHT_GROUPS))[LAYER_0_GROUPS:]:
                a, z = WEIGHT_COLS[first][0], sum(WEIGHT_COLS[last])
                sp.dma_start(g.weights[:, a:z], ins["weights"][:, LAYER_WIDTH + a:LAYER_WIDTH + z])\
                    .then_inc(g.weights_loaded[n], 16)


def norm_stage(nc, g, tag, source, out, center, mean, chunks=B, width=T):
    with ExitStack() as ctx:
        sem = ctx.enter_context(semaphores(nc, tag))
        sq = ctx.enter_context(nc.sbuf_tensor(f"{tag}_sq", [D, chunks, width], fp32))
        xc = ctx.enter_context(nc.sbuf_tensor(f"{tag}_xc", [D, chunks, width], fp32))
        sd = ctx.enter_context(nc.sbuf_tensor(f"{tag}_sd", [D, chunks, width], fp32))
        centered, squared, varied = sem("centered"), sem("squared"), sem("varied")
        copied, rooted, logged, done = sem("copied"), sem("rooted"), sem("logged"), sem("done")
        with nc.Block() as block:
            @block.tensor
            def _(pe):
                pe.wait_ge(g.x_loaded, 16)
                pe.wait_ge(g.const_loaded, 16)
                pe.wait_ge(g.ctx_loaded, 32)
                for b in range(chunks):
                    nc.tensor.matmul(g.ps[:, b, 0:width], g.c(center), source(b), start=True, stop=True)\
                        .then_inc(centered, 1)
                for b in range(chunks):
                    pe.wait_ge(squared, b + 1)
                    nc.tensor.matmul(g.ps[:, B + b, 0:width], g.c(mean), sq[:, b, :], start=True, stop=True)\
                        .then_inc(varied, 1)

            @block.scalar
            def _(act):
                for b in range(chunks):
                    act.wait_ge(centered, b + 1)
                    act.wait_ge(copied, b + 1)
                    nc.scalar.activation(sq[:, b, :], g.ps[:, b, 0:width], ACT.Square).then_inc(squared, 1)
                for b in range(chunks):
                    act.wait_ge(varied, b + 1)
                    nc.scalar.activation(sd[:, b, :], g.ps[:, B + b, 0:width], ACT.Ln, bias=g.eps[:, :])\
                        .then_inc(logged, 1)
                for b in range(chunks):
                    act.wait_ge(logged, b + 1)
                    nc.scalar.activation(sd[:, b, :], sd[:, b, :], ACT.Exp, scale=-0.5).then_inc(rooted, 1)

            @block.vector
            def _(dve):
                for b in range(chunks):
                    dve.wait_ge(centered, b + 1)
                    nc.vector.tensor_copy(xc[:, b, :], g.ps[:, b, 0:width]).then_inc(copied, 1)
                for b in range(chunks):
                    dve.wait_ge(rooted, b + 1)
                    nc.vector.tensor_tensor(out(b), xc[:, b, :], sd[:, b, :], ALU.mult).then_inc(done, 1)


def rwkv_stage(nc, g):
    with ExitStack() as ctx:
        sem = ctx.enter_context(semaphores(nc, "rw"))

        def sb(name, shape):
            return ctx.enter_context(nc.sbuf_tensor(f"rw_{name}", shape, fp32))
        xn = sb("xn", [D, B, T + 1])
        o = sb("o", [D, B, T])
        r = sb("r", [D, B, T])
        zeroed = sem("zeroed")
        with nc.Block() as block:
            @block.gpsimd
            def _(pool):
                nc.gpsimd.memset(xn[:, :, 0:1], 0.0).then_inc(zeroed, 1)
                nc.gpsimd.memset(g.eps[:, :], EPS).then_inc(zeroed, 1)
        norm_stage(nc, g, "rwln", lambda b: g.x[:, bass.ts(b, T)], lambda b: xn[:, b, 1:T + 1],
                   "center", "mean")
        with ExitStack() as inner:
            def isb(name, shape):
                return inner.enter_context(nc.sbuf_tensor(f"rw_{name}", shape, fp32))
            a, k, xv, vc = (isb(n, [D, B, T]) for n in ("a", "k", "xv", "vc"))
            dx = isb("dx", [D, 2, T])
            mix = isb("mix", [D, 2, 3, T])
            eu = isb("eu", [D, 2, T])
            vsb = isb("vsb", [D, 2, T])
            kv = isb("kv", [D, 2, T])
            state = isb("state", [D, 2, T + 1])
            rs = isb("rs", [D, 2, T])
            diffed, mixed, projected = sem("diffed"), sem("mixed"), sem("projected")
            evacuated, scaled, bonus_in, bonus, bonused = (
                sem(n) for n in ("evacuated", "scaled", "bonus_in", "bonus", "bonused"))
            vrepped, multiplied, scanned, read, summed, added, zero = (
                sem(n) for n in ("vrepped", "multiplied", "scanned", "read", "summed", "added", "zero"))
            BANK = {"r": 0, "k": 1, "w": 2, "v": 3}
            with nc.Block() as block:
                @block.tensor
                def _(pe):
                    pe.wait_ge(g.weights_loaded[0], 16)
                    for b in range(B):
                        for n, name in enumerate("rkwv"):
                            pe.wait_ge(mixed, 4 * b + n + 1)
                            if b:
                                pe.wait_ge(evacuated, 5 * (b - 1) + (1, 3, 4, 5)[n])
                            rhs = xv[:, b, :] if name == "v" else mix[:, b % 2, n, :]
                            nc.tensor.matmul(g.ps[:, n, :], g.w(name), rhs, start=True, stop=True)\
                                .then_inc(projected, 1)
                        pe.wait_ge(bonus_in, b + 1)
                        if b >= 2:
                            pe.wait_ge(bonused, b - 1)
                        nc.tensor.matmul(g.ps[:, 4 + b % 2, :], g.c("hsum"), eu[:, b % 2, :],
                                         start=True, stop=True).then_inc(bonus, 1)

                @block.scalar
                def _(act):
                    act.wait_ge(g.vec_loaded, 16)
                    for b in range(B):
                        act.wait_ge(projected, 4 * b + 1)
                        nc.scalar.activation(r[:, b, :], g.ps[:, 0, :], ACT.Tanh, scale=0.5)\
                            .then_inc(evacuated, 1)
                        act.wait_ge(projected, 4 * b + 2)
                        nc.scalar.activation(k[:, b, :], g.ps[:, 1, :], ACT.Identity).then_inc(evacuated, 1)
                        if b >= 2:
                            act.wait_ge(bonus, b - 1)
                        nc.scalar.activation(eu[:, b % 2, :], g.ps[:, 1, :], ACT.Exp, bias=g.v("u"))\
                            .then_inc(evacuated, 1)
                        act.wait_ge(projected, 4 * b + 3)
                        nc.scalar.activation(a[:, b, :], g.ps[:, 2, :], ACT.Tanh, scale=0.5)\
                            .then_inc(evacuated, 1)
                        act.wait_ge(projected, 4 * b + 4)
                        if b >= 2:
                            act.wait_ge(bonused, b - 1)
                        nc.scalar.activation(vsb[:, b % 2, :], g.ps[:, 3, :], ACT.Identity)\
                            .then_inc(evacuated, 1)

                @block.gpsimd
                def _(pool):
                    for b in range(B):
                        pool.wait_ge(evacuated, 5 * b + 3)
                        nc.gpsimd.tensor_scalar(r[:, b, :], r[:, b, :], 0.5, 0.5, ALU.mult, ALU.add)\
                            .then_inc(scaled, 1)
                        pool.wait_ge(scaled, 2 * b + 1)
                        nc.gpsimd.tensor_tensor(eu[:, b % 2, :], eu[:, b % 2, :], r[:, b, :], ALU.mult)\
                            .then_inc(bonus_in, 1)
                        pool.wait_ge(evacuated, 5 * b + 4)
                        c = float(0.5 * np.exp(-0.0001))
                        nc.gpsimd.tensor_scalar(a[:, b, :], a[:, b, :], c, c, ALU.mult, ALU.add)\
                            .then_inc(scaled, 1)

                @block.vector
                def _(dve):
                    dve.wait_ge(g.vec_loaded, 16)
                    for b in range(B):
                        if b >= 2:
                            dve.wait_ge(projected, 4 * (b - 1))
                        nc.vector.tensor_tensor(dx[:, b % 2, :], xn[:, b, 1:T + 1], xn[:, b, 0:T],
                                                ALU.subtract).then_inc(diffed, 1)
                        dve.wait_ge(diffed, b + 1)
                        for n, name in enumerate("rkwv"):
                            to = xv[:, b, :] if name == "v" else mix[:, b % 2, n, :]
                            nc.vector.scalar_tensor_tensor(out=to, in0=dx[:, b % 2, :], scalar=g.v("tm_" + name),
                                                           in1=xn[:, b, 0:T], op0=ALU.mult, op1=ALU.add)\
                                .then_inc(mixed, 1)
                        if b:
                            dve.wait_ge(bonus, b)
                            dve.wait_ge(evacuated, 5 * b)
                            nc.vector.tensor_tensor(vc[:, b - 1, :], g.ps[:, 4 + (b - 1) % 2, :],
                                                    vsb[:, (b - 1) % 2, :], ALU.mult).then_inc(bonused, 1)
                    dve.wait_ge(bonus, B)
                    dve.wait_ge(evacuated, 5 * B)
                    nc.vector.tensor_tensor(vc[:, B - 1, :], g.ps[:, 4 + (B - 1) % 2, :],
                                            vsb[:, (B - 1) % 2, :], ALU.mult).then_inc(bonused, 1)
            with nc.Block() as block:
                @block.tensor
                def _(pe):
                    def sum_heads(n):
                        b, j = divmod(n, HD)
                        pe.wait_ge(read, n + 1)
                        if j == 0 and b >= 2:
                            pe.wait_ge(added, b - 1)
                        at = CONST_COLS["hsel"][0] + j * D
                        nc.tensor.matmul(g.ps[:, 2 + b % 2, :], g.const[:, at:at + D], rs[:, n % 2, :],
                                         start=j == 0, stop=j == HD - 1).then_inc(summed, 1)
                    for n in range(B * HD):
                        b, j = divmod(n, HD)
                        if n >= 2:
                            pe.wait_ge(multiplied, n - 1)
                        at = WEIGHT_COLS["vrep"][0] + j * D
                        nc.tensor.matmul(g.ps[:, n % 2, :], g.weights[:, at:at + D], xv[:, b, :],
                                         start=True, stop=True).then_inc(vrepped, 1)
                        if n >= 2:
                            sum_heads(n - 2)
                    sum_heads(B * HD - 2)
                    sum_heads(B * HD - 1)

                @block.vector
                def _(dve):
                    nc.vector.memset(state[:, :, 0:1], 0.0).then_inc(zero, 1)

                    def multiply(n):
                        dve.wait_ge(vrepped, n + 1)
                        if n >= 2:
                            dve.wait_ge(scanned, n - 1)
                        nc.vector.tensor_tensor(kv[:, n % 2, :], g.ps[:, n % 2, :], k[:, n // HD, :],
                                                ALU.mult).then_inc(multiplied, 1)
                    multiply(0)
                    for n in range(B * HD):
                        b, j = divmod(n, HD)
                        if n + 1 < B * HD:
                            multiply(n + 1)
                        dve.wait_ge(multiplied, n + 1)
                        if n >= 2:
                            dve.wait_ge(read, n - 1)
                        nc.vector.tensor_tensor_scan(state[:, n % 2, 1:T + 1], a[:, b, :], kv[:, n % 2, :],
                                                     0.0, ALU.mult, ALU.add).then_inc(scanned, 1)
                        if j == 4 and b:
                            dve.wait_ge(summed, HD * b)
                            nc.vector.tensor_tensor(o[:, b - 1, :], g.ps[:, 2 + (b - 1) % 2, :],
                                                    vc[:, b - 1, :], ALU.add).then_inc(added, 1)
                    dve.wait_ge(summed, HD * B)
                    nc.vector.tensor_tensor(o[:, B - 1, :], g.ps[:, 2 + (B - 1) % 2, :],
                                            vc[:, B - 1, :], ALU.add).then_inc(added, 1)

                @block.gpsimd
                def _(pool):
                    pool.wait_ge(zero, 1)
                    for n in range(B * HD):
                        pool.wait_ge(scanned, n + 1)
                        if n >= 2:
                            pool.wait_ge(summed, n - 1)
                        nc.gpsimd.tensor_tensor(rs[:, n % 2, :], state[:, n % 2, 0:T], r[:, n // HD, :],
                                                ALU.mult).then_inc(read, 1)
        norm_stage(nc, g, "rwgn", lambda b: o[:, b, :], lambda b: o[:, b, :], "hcenter", "hmean")
        gated, affine, out_ready = sem("gated"), sem("affine"), sem("out_ready")
        added_x = sem("added_x")
        with nc.Block() as block:
            @block.vector
            def _(dve):
                for b in range(B):
                    nc.vector.tensor_scalar(o[:, b, :], o[:, b, :], g.v("ln_w"), g.v("ln_b"),
                                            ALU.mult, ALU.add).then_inc(affine, 1)
                    dve.wait_ge(affine, b + 1)
                    nc.vector.tensor_tensor(o[:, b, :], o[:, b, :], r[:, b, :], ALU.mult).then_inc(gated, 1)
                for b in range(B):
                    dve.wait_ge(out_ready, b + 1)
                    nc.vector.tensor_tensor(g.x[:, bass.ts(b, T)], g.ps[:, b, :], g.x[:, bass.ts(b, T)],
                                            ALU.add).then_inc(added_x, 1)

            @block.tensor
            def _(pe):
                for b in range(B):
                    pe.wait_ge(gated, b + 1)
                    nc.tensor.matmul(g.ps[:, b, :], g.w("o"), o[:, b, :], start=True, stop=True)\
                        .then_inc(out_ready, 1)


def xattn_stage(nc, g):
    NTILE = NT // 128
    with ExitStack() as ctx:
        sem = ctx.enter_context(semaphores(nc, "xa"))

        def sb(name, shape):
            return ctx.enter_context(nc.sbuf_tensor(f"xa_{name}", shape, fp32))
        xn = sb("xn", [D, B, T])
        norm_stage(nc, g, "xaln", lambda b: g.x[:, bass.ts(b, T)], lambda b: xn[:, b, :], "center", "mean")
        q, k = sb("q", [D, B, T]), sb("k", [D, B * LC])
        nmax, total = sb("nmax", [128, NTILE]), sb("total", [128, NTILE])
        p = sb("p", [128, NTILE, LC])
        pT = sb("pT", [LC, B, T])
        k_proj, q_proj, k_ready, q_ready, scored, maxed, lowered, exped, totalled, inverted, normed = (
            sem(n) for n in ("k_proj", "q_proj", "k_ready", "q_ready", "scored", "maxed", "lowered", "exped",
                             "totalled", "inverted", "normed"))
        turned, pT_ready, attended, added = (sem(n) for n in ("turned", "pT_ready", "attended", "added"))
        scores = g.ps[:, 5, :].rearrange("p (n c) -> p n c", c=LC)
        with nc.Block() as block:
            @block.tensor
            def _(pe):
                pe.wait_ge(g.weights_loaded[1], 16)
                pe.wait_ge(g.ctx_loaded, 32)
                nc.tensor.matmul(g.ps[:, 4, 0:B * LC], g.w("xk"), g.ctxT[:, :], start=True, stop=True)\
                    .then_inc(k_proj, 1)
                for b in range(B):
                    nc.tensor.matmul(g.ps[:, b, :], g.w("xq"), xn[:, b, :], start=True, stop=True)\
                        .then_inc(q_proj, 1)
                pe.wait_ge(k_ready, 1)
                for n in range(NTILE):
                    b, t = divmod(n, QT)
                    if t == 0:
                        pe.wait_ge(q_ready, b + 1)
                    last = nc.tensor.matmul(scores[:, n, :], q[:, b, bass.ts(t, 128)],
                                            k[:, bass.ts(b, LC)], start=True, stop=True)
                last.then_inc(scored, 1)
                pe.wait_ge(normed, 1)
                for n in range(NTILE):
                    b, t = divmod(n, QT)
                    last = nc.tensor.transpose(g.ps[0:LC, b, bass.ts(t, 128)], p[:, n, :], g.c("ident"))
                    if t == QT - 1:
                        last.then_inc(turned, 1)
                for b in range(B):
                    pe.wait_ge(pT_ready, b + 1)
                    nc.tensor.matmul(g.ps[:, b, :], g.ctx[:, b, :], pT[:, b, :], start=True, stop=True)\
                        .then_inc(attended, 1)

            @block.scalar
            def _(act):
                act.wait_ge(k_proj, 1)
                nc.scalar.activation(k[:, :], g.ps[:, 4, 0:B * LC], ACT.Identity, bias=g.v("bk")).then_inc(k_ready, 1)
                for b in range(B):
                    act.wait_ge(q_proj, b + 1)
                    nc.scalar.activation(q[:, b, :], g.ps[:, b, :], ACT.Identity, bias=g.v("bq")).then_inc(q_ready, 1)
                act.wait_ge(lowered, 1)
                nc.scalar.activation(p[:, :, :], p[:, :, :], ACT.Exp, scale=1.0 / 32.0).then_inc(exped, 1)
                for b in range(B):
                    act.wait_ge(turned, b + 1)
                    nc.scalar.activation(pT[:, b, :], g.ps[0:LC, b, :], ACT.Identity).then_inc(pT_ready, 1)

            @block.vector
            def _(dve):
                dve.wait_ge(scored, 1)
                nc.vector.tensor_reduce(nmax[:, :], scores, AX.X, ALU.max, negate=True).then_inc(maxed, 1)
                dve.wait_ge(maxed, 1)
                nc.vector.tensor_tensor(p[:, :, :], scores, nmax[:, :].unsqueeze(2).broadcast_to([128, NTILE, LC]),
                                        ALU.add).then_inc(lowered, 1)
                dve.wait_ge(exped, 1)
                nc.vector.tensor_reduce(total[:, :], p[:, :, :], AX.X, ALU.add).then_inc(totalled, 1)
                dve.wait_ge(totalled, 1)
                nc.vector.reciprocal(total[:, :], total[:, :]).then_inc(inverted, 1)
                dve.wait_ge(inverted, 1)
                nc.vector.tensor_tensor(p[:, :, :], p[:, :, :],
                                        total[:, :].unsqueeze(2).broadcast_to([128, NTILE, LC]), ALU.mult)\
                    .then_inc(normed, 1)
                for b in range(B):
                    dve.wait_ge(attended, b + 1)
                    nc.vector.tensor_tensor(g.x[:, bass.ts(b, T)], g.ps[:, b, :], g.x[:, bass.ts(b, T)],
                                            ALU.add).then_inc(added, 1)


Q_PARTS = (0, 0, 1, 0, 1, 2)
K_PARTS = (0, 1, 0, 2, 1, 0)
TERM_ROWS = HD * len(Q_PARTS)
UH = 8
UNITS = B * H // UH
LAG = 2


def join_heads_stage(nc, g, tag, osum, o):
    with ExitStack() as ctx:
        sem = ctx.enter_context(semaphores(nc, f"{tag}j"))
        rsum = ctx.enter_context(nc.sbuf_tensor(f"{tag}_rsum", [128, T], fp32))
        spread = ctx.enter_context(nc.sbuf_tensor(f"{tag}_spread", [D, 2, T], fp32))
        summed, inverted, densed, spreaded, copied, divided = (
            sem(n) for n in ("summed", "inverted", "densed", "spreaded", "copied", "divided"))
        with nc.Block() as block:
            @block.tensor
            def _(pe):
                for b in range(B):
                    for grp in range(4):
                        last = nc.tensor.matmul(g.ps[32 * b:32 * b + 32, 0, :], g.c(f"sums{grp}"),
                                                osum[:, b, grp, :], start=grp == 0, stop=grp == 3)
                last.then_inc(summed, 1)
                for b in range(B):
                    if b >= 2:
                        pe.wait_ge(divided, b - 1)
                    for grp in range(4):
                        last = nc.tensor.matmul(g.ps[:, 1 + b % 2, :], g.c(f"dense{grp}"), osum[:, b, grp, :],
                                                start=grp == 0, stop=grp == 3)
                    last.then_inc(densed, 1)
                    if b == 0:
                        pe.wait_ge(inverted, 1)
                    if b >= 2:
                        pe.wait_ge(copied, b - 1)
                    nc.tensor.matmul(g.ps[:, 3 + b % 2, :], g.c("spread")[32 * b:32 * b + H, :],
                                     rsum[32 * b:32 * b + H, :], start=True, stop=True).then_inc(spreaded, 1)

            @block.scalar
            def _(act):
                for b in range(B):
                    act.wait_ge(spreaded, b + 1)
                    if b >= 2:
                        act.wait_ge(divided, b - 1)
                    nc.scalar.activation(spread[:, b % 2, :], g.ps[:, 3 + b % 2, :], ACT.Identity)\
                        .then_inc(copied, 1)

            @block.vector
            def _(dve):
                dve.wait_ge(summed, 1)
                nc.vector.reciprocal(rsum[:, :], g.ps[:, 0, :]).then_inc(inverted, 1)
                for b in range(B):
                    dve.wait_ge(densed, b + 1)
                    dve.wait_ge(copied, b + 1)
                    nc.vector.tensor_tensor(o[:, b, :], g.ps[:, 1 + b % 2, :], spread[:, b % 2, :], ALU.mult)\
                        .then_inc(divided, 1)


def attention_stage(nc, g, tag, xn, wq, wk, wv, group, scale, o, causal=False, classes=None, keep=None):
    KS = TERM_ROWS + (2 if classes else 0)
    KT = KS + 3
    with ExitStack() as ctx:
        sem = ctx.enter_context(semaphores(nc, tag))

        def sb(name, shape, dt=fp32):
            return ctx.enter_context(nc.sbuf_tensor(f"{tag}_{name}", shape, dt))
        v9 = sb("v9", [128, B * QT, H, HD + 1])
        parts_dram = nc.dram_tensor(f"{tag}_parts", [B, 2, 3, D, T], bf16, kind="Internal").ap()
        parts_written = [sem(f"parts_written_{n}") for n in range(2)]
        NBUF = 4
        qst = sb("qst", [128, NBUF, UH, T], bf16)
        kst = sb("kst", [128, NBUF, UH, T], bf16)
        cleared = sem("cleared")
        with ExitStack() as inner:
            parts = inner.enter_context(nc.sbuf_tensor(f"{tag}_qkparts", [D, 2, 2, 3, T], bf16))
            rest = inner.enter_context(nc.sbuf_tensor(f"{tag}_rest", [D, 2, 2, T], fp32))
            projected, first, second, third, left, v_out, one = (
                sem(n) for n in ("projected", "first", "second", "third", "left", "v_out", "one"))
            with nc.Block() as block:
                @block.tensor
                def _(pe):
                    pe.wait_ge(g.weights_loaded[group], 16)
                    for b in range(B):
                        for s, w in enumerate((wq, wk)):
                            if b >= 2:
                                pe.wait_ge(left, 2 * (b - 2) + s + 1)
                            nc.tensor.matmul(g.ps[:, 2 * s + b % 2, :], w, xn[:, b, :], start=True, stop=True)\
                                .then_inc(projected, 1)
                        if b >= 2:
                            pe.wait_ge(v_out, b - 1)
                        for t in range(QT):
                            last = nc.tensor.matmul(g.ps[:, 4 + b % 2, bass.ts(t, 128)],
                                                    xn[:, b, bass.ts(t, 128)], wv, start=True, stop=True)
                        last.then_inc(projected, 1)

                @block.scalar
                def _(act):
                    for b in range(B):
                        for s in range(2):
                            act.wait_ge(projected, 3 * b + s + 1)
                            if b >= 2:
                                act.wait_ge(parts_written[b % 2], 32 * (b // 2))
                            nc.scalar.activation(parts[:, b % 2, s, 0, :], g.ps[:, 2 * s + b % 2, :], ACT.Identity,
                                                 scale=scale if s == 0 else 1.0).then_inc(first, 1)
                        for s in range(2):
                            act.wait_ge(left, 2 * b + s + 1)
                            nc.scalar.activation(parts[:, b % 2, s, 1, :], rest[:, b % 2, s, :], ACT.Identity)\
                                .then_inc(second, 1)
                        act.wait_ge(projected, 3 * b + 3)
                        nc.scalar.activation(
                            v9[:, QT * b:QT * b + QT, :, 0:HD],
                            g.ps[:, 4 + b % 2, :].rearrange("p (t h d) -> p t h d", t=QT, d=HD), ACT.Identity)\
                            .then_inc(v_out, 1)

                @block.vector
                def _(dve):
                    for b in range(B):
                        for s in range(2):
                            dve.wait_ge(first, 2 * b + s + 1)
                            nc.vector.scalar_tensor_tensor(
                                out=rest[:, b % 2, s, :], in0=g.ps[:, 2 * s + b % 2, :],
                                scalar=scale if s == 0 else 1.0, in1=parts[:, b % 2, s, 0, :],
                                op0=ALU.mult, op1=ALU.subtract).then_inc(left, 1)
                        for s in range(2):
                            dve.wait_ge(second, 2 * b + s + 1)
                            nc.vector.tensor_tensor(parts[:, b % 2, s, 2, :], rest[:, b % 2, s, :],
                                                    parts[:, b % 2, s, 1, :], ALU.subtract).then_inc(third, 1)

                @block.gpsimd
                def _(pool):
                    nc.gpsimd.memset(v9[:, :, :, HD:HD + 1], 1.0).then_inc(one, 1)
                    nc.gpsimd.memset(qst[:, 0, :, :], 0.0).then_inc(cleared, 1)
                    nc.gpsimd.memset(kst[:, 0, :, :], 0.0).then_inc(cleared, 1)

                @block.sync
                def _(sp):
                    for b in range(B):
                        for s in range(2):
                            sp.wait_ge(third, 2 * b + s + 1)
                            sp.dma_start(parts_dram[b, s].rearrange("n c t -> c n t"), parts[:, b % 2, s, :, :])\
                                .then_inc(parts_written[b % 2], 16)
                    for n in range(2):
                        sp.wait_ge(parts_written[n], 32 * (B // 2))
        osum = sb("osum", [128, B, H // 4, T])
        with ExitStack() as inner:
            def isb(name, shape, dt=fp32):
                return inner.enter_context(nc.sbuf_tensor(f"{tag}_{name}", shape, dt))
            weights_t = isb("pt", [128, 2, 2 * T])
            vst = isb("vst", [128, 4, QT, 32])
            nmax = isb("nmax", [128, UH, QT])
            mrest = isb("mrest", [128, 2, UH, QT])
            mparts = isb("mparts", [128, 2, QT, 3, UH], bf16)
            mrows = isb("mrows", [3 * UH, 2, T], bf16)
            (stack_loaded, m_loaded, scored, maxed, split1, split2, split3, split4, m_turned, m_ready,
             st_scored, exped, pv_done, vst_ready, o_out) = (sem(n) for n in (
                 "stack_loaded", "m_loaded", "scored", "maxed", "split1", "split2", "split3", "split4",
                 "m_turned", "m_ready", "st_scored", "exped", "pv_done", "vst_ready", "o_out"))
            LOADS = 2 + 2 * len(Q_PARTS) + (classes["loads"] if classes else 0)

            def keys_of(qt):
                return (qt + 1) * 128 if causal else T

            def first_query(kt):
                return kt * 128 if causal else 0

            def column(kt):
                return 0 if kt % 2 == 0 else T - first_query(kt - 1)

            def width(pair):
                return column(2 * pair + 1) + T - first_query(2 * pair + 1)

            def buf(b, half):
                return (b % 2) * 2 + half

            with nc.Block() as block:
                def phases(eng, step):
                    for half in range(2):
                        step(eng, (0, half), None)
                    for b in range(1, B):
                        for half in range(2):
                            step(eng, (b, half), (b - 1, half))
                    for half in range(2):
                        step(eng, None, (B - 1, half))

                @block.sync
                def _(sp):
                    def load_stack(b, half):
                        h0 = half * UH
                        at = buf(b, half)
                        for s, (stack, order) in enumerate(((qst, Q_PARTS), (kst, K_PARTS))):
                            for n, part in enumerate(order):
                                src = parts_dram[b, s, part, h0 * HD:(h0 + UH) * HD, :]
                                dst = stack[n * HD:(n + 1) * HD, bass.ds(at, 1), :, :]\
                                    .rearrange("d b h t -> d (b h) t")
                                sp.dma_start(dst, src.rearrange("(h d) t -> d h t", d=HD))\
                                    .then_inc(stack_loaded, 16)
                        sp.dma_start(kst[KS:KT, at, :, :], g.ones_dram).then_inc(stack_loaded, 16)
                        sp.dma_start(qst[KS:KT, at, :, :], g.zeros_dram).then_inc(stack_loaded, 16)
                        if classes:
                            classes["load"](sp, qst, kst, b, at, stack_loaded)

                    def load_maxima(b, half):
                        u = 2 * b + half
                        sp.wait_ge(m_ready, u + 1)
                        for n in range(3):
                            dst = qst[KS + n:KS + n + 1, bass.ds(buf(b, half), 1), :, :]\
                                .rearrange("r b h t -> r (b h) t")
                            sp.dma_start(dst, mrows[n * UH:(n + 1) * UH, half, :]).then_inc(m_loaded, 16)
                        sp.wait_ge(m_loaded, 48 * (u + 1))

                    for b in range(2):
                        for half in range(2):
                            sp.wait_ge(cleared, 2 * (2 * b + half + 1))
                            load_stack(b, half)
                            sp.wait_ge(stack_loaded, 16 * LOADS * (2 * b + half + 1))
                    for half in range(2):
                        load_maxima(0, half)
                    for b in range(1, B - 1):
                        for half in range(2):
                            load_maxima(b, half)
                            sp.wait_ge(st_scored, 2 * UH * (2 * b + half - 1))
                            load_stack(b + 1, half)
                            sp.wait_ge(stack_loaded, 16 * LOADS * (2 * b + half + 3))
                    for half in range(2):
                        load_maxima(B - 1, half)

                @block.gpsimd
                def _(pool):
                    nc.gpsimd.memset(vst[:, :, :, :], 0.0).then_inc(vst_ready, 1)
                    for n in range(1, NBUF):
                        nc.gpsimd.memset(qst[:, n, :, :], 0.0).then_inc(cleared, 1)
                        nc.gpsimd.memset(kst[:, n, :, :], 0.0).then_inc(cleared, 1)
                    pool.wait_ge(vst_ready, 1)

                    def copy_values(b, half):
                        for h in range(UH):
                            n = (2 * b + half) * UH + h
                            if n >= 4:
                                pool.wait_ge(pv_done, 2 * n - 6)
                            src = v9[:, bass.ds(b * QT, QT), half * UH + h, :]
                            nc.gpsimd.tensor_copy(vst[:, h % 4, :, 0:HD + 1], src).then_inc(vst_ready, 1)
                    for half in range(2):
                        copy_values(0, half)
                    for b in range(1, B):
                        for half in range(2):
                            copy_values(b, half)

                @block.tensor
                def _(pe):
                    def score(b, half, h, qt):
                        n = ((2 * b + half) * UH + h) * QT + qt
                        if n >= 2:
                            pe.wait_ge(maxed, n - 1)
                        if h == 1 and qt == 0 and b + half > 0:
                            pe.wait_ge(m_ready, 2 * b + half)
                        at, keys = buf(b, half), keys_of(qt)
                        q = qst[:, bass.ds(at, 1), h, bass.ts(qt, 128)].rearrange("k b t -> k (b t)")
                        k = kst[:, bass.ds(at, 1), h, 0:keys].rearrange("k b t -> k (b t)")
                        last = nc.tensor.matmul(g.ps[:, qt % 2, 0:keys], q, k, start=True, stop=not causal)
                        if causal:
                            last = nc.tensor.matmul(g.ps[:, qt % 2, bass.ts(qt, 128)], g.ident_bf[:, :],
                                                    g.lowered_bf[:, :], start=False, stop=True)
                        last.then_inc(scored, 1)

                    def turn_maxima(b, half, next_s):
                        u = 2 * b + half
                        pe.wait_ge(split4, u + 1)
                        if next_s:
                            pe.wait_ge(maxed, (u + 1) * UH * QT + 3)
                        for qt in range(QT):
                            last = nc.tensor.matmul(g.ps[0:3 * UH, 0, bass.ts(qt, 128)],
                                                    mparts[:, half, qt, :, :].rearrange("p n h -> p (n h)"),
                                                    g.ident_bf[:, :], start=True, stop=True)
                        last.then_inc(m_turned, 1)

                    def score_t(b, half, h, pair):
                        n = ((2 * b + half) * UH + h) * 2 + pair
                        if h == 0 and pair == 0:
                            pe.wait_ge(m_loaded, 48 * (2 * b + half + 1))
                        if n >= 2:
                            pe.wait_ge(exped, n - 1)
                        at = buf(b, half)
                        for kt in (2 * pair, 2 * pair + 1):
                            q0 = first_query(kt)
                            c = column(kt)
                            bank, c = 2 + 2 * pair + c // T, c % T
                            q = qst[:, bass.ds(at, 1), h, q0:T].rearrange("k b t -> k (b t)")
                            k = kst[:, bass.ds(at, 1), h, bass.ts(kt, 128)].rearrange("k b t -> k (b t)")
                            last = nc.tensor.matmul(g.ps[:, bank, c:c + T - q0], k, q, start=True, stop=not causal)
                            if causal:
                                last = nc.tensor.matmul(g.ps[:, bank, c:c + 128], g.ident_bf[:, :],
                                                        g.loweredT_bf[:, :], start=False, stop=True)
                        last.then_inc(st_scored, 1)

                    def values(n, pair):
                        j, grp = n % UH, n // 4
                        pe.wait_ge(exped, 2 * n + pair + 1)
                        if pair == 0:
                            pe.wait_ge(vst_ready, n + 2)
                            if j % 4 == 0 and grp >= 2:
                                pe.wait_ge(o_out, grp - 1)
                        for kt in (2 * pair, 2 * pair + 1):
                            q0, c = first_query(kt), column(kt)
                            last = nc.tensor.matmul(g.ps[32 * (j % 4):32 * (j % 4) + 32, 6 + j // 4, q0:T],
                                                    vst[:, j % 4, kt, :], weights_t[:, pair, c:c + T - q0],
                                                    start=kt == 0, stop=kt == QT - 1)
                        last.then_inc(pv_done, 1)

                    def step(pe, s, t):
                        if s:
                            pe.wait_ge(stack_loaded, 16 * LOADS * (2 * s[0] + s[1] + 1))
                        for h in range(UH):
                            n = (2 * t[0] + t[1]) * UH + h if t else 0
                            if s:
                                score(*s, h, 0)
                                score(*s, h, 1)
                            if t:
                                score_t(*t, h, 0)
                                if n > 0:
                                    values(n - 1, 1)
                            if s:
                                score(*s, h, 2)
                                score(*s, h, 3)
                            if h == 0:
                                if s and s[0] + s[1] > 0:
                                    if s[1] == 1:
                                        turn_maxima(s[0], 0, True)
                                    else:
                                        turn_maxima(s[0] - 1, 1, True)
                                elif not s and t[1] == 0:
                                    turn_maxima(B - 1, 1, False)
                            if t:
                                score_t(*t, h, 1)
                                values(n, 0)
                    phases(pe, step)
                    values(B * H - 1, 1)

                @block.vector
                def _(dve):
                    def step(dve, s, t):
                        if not s:
                            return
                        b, half = s
                        for h in range(UH):
                            for qt in range(QT):
                                dve.wait_ge(scored, ((2 * b + half) * UH + h) * QT + qt + 1)
                                nc.vector.tensor_reduce(nmax[:, h, qt:qt + 1], g.ps[:, qt % 2, 0:keys_of(qt)],
                                                        AX.X, ALU.max, negate=True).then_inc(maxed, 1)
                        u = 2 * b + half
                        dve.wait_ge(maxed, (u + 1) * UH * QT)
                        if b > 0:
                            dve.wait_ge(m_turned, u - 1)
                        part = lambda n: mparts[:, half, :, n, :].rearrange("p q h -> p h q")
                        nc.vector.tensor_copy(part(0), nmax[:, :, :]).then_inc(split1, 1)
                        dve.wait_ge(split1, u + 1)
                        nc.vector.tensor_tensor(mrest[:, 0, :, :], nmax[:, :, :], part(0), ALU.subtract)\
                            .then_inc(split2, 1)
                        dve.wait_ge(split2, u + 1)
                        nc.vector.tensor_copy(part(1), mrest[:, 0, :, :]).then_inc(split3, 1)
                        dve.wait_ge(split3, u + 1)
                        nc.vector.tensor_tensor(part(2), mrest[:, 0, :, :], part(1), ALU.subtract)\
                            .then_inc(split4, 1)
                    phases(dve, step)

                @block.scalar
                def _(act):
                    def copy_maxima(b, half):
                        u = 2 * b + half
                        act.wait_ge(m_turned, u + 1)
                        if u >= 2:
                            act.wait_ge(m_loaded, 48 * (u - 1))
                        nc.scalar.activation(mrows[:, half, :], g.ps[0:3 * UH, 0, :], ACT.Identity)\
                            .then_inc(m_ready, 1)

                    def copy_output(b, half, grp):
                        n = (2 * b + half) * 2 + grp
                        act.wait_ge(pv_done, 8 * (n + 1))
                        to = osum[:, bass.ds(b, 1), 2 * half + grp, :].rearrange("p b t -> p (b t)")
                        nc.scalar.activation(to, g.ps[:, 6 + grp, :], ACT.Identity).then_inc(o_out, 1)

                    def step(act, s, t):
                        for h in range(UH):
                            if t:
                                b, half = t
                                n = ((2 * b + half) * UH + h) * 2
                                for pair in range(2):
                                    act.wait_ge(st_scored, n + pair + 1)
                                    if n >= 2:
                                        act.wait_ge(pv_done, n + pair - 1)
                                    nc.scalar.activation(
                                        weights_t[:, pair, 0:width(pair)],
                                        g.ps[:, 2 + 2 * pair:4 + 2 * pair, :]
                                        .rearrange("p b t -> p (b t)")[:, 0:width(pair)], ACT.Exp).then_inc(exped, 1)
                                    if pair == 0 and h == 4:
                                        copy_output(b, half, 0)
                                    if pair == 0 and h == 0:
                                        if half == 1:
                                            copy_output(b, 0, 1)
                                        elif b > 0:
                                            copy_output(b - 1, 1, 1)
                                    if pair == 0 and h == 0:
                                        turn = None
                                        if s:
                                            turn = (s[0], 0) if s[1] == 1 else (s[0] - 1, 1)
                                        elif half == 0:
                                            turn = (B - 1, 1)
                                        if turn:
                                            copy_maxima(*turn)
                            elif h == 0 and s[1] == 1:
                                copy_maxima(s[0], 0)
                    phases(act, step)
                    copy_output(B - 1, 1, 1)

        join_heads_stage(nc, g, tag, osum, o)


def rms_add_stage(nc, g, tag, product, weight, base, out, y=None):
    with ExitStack() as ctx:
        sem = ctx.enter_context(semaphores(nc, tag))
        sq = ctx.enter_context(nc.sbuf_tensor(f"{tag}_sq", [D, B, T], fp32))
        if product:
            y = ctx.enter_context(nc.sbuf_tensor(f"{tag}_y", [D, B, T], fp32))
        made, copied, squared, averaged, logged, rooted, scaled, added = (
            sem(n) for n in ("made", "copied", "squared", "averaged", "logged", "rooted", "scaled", "added"))
        with nc.Block() as block:
            @block.tensor
            def _(pe):
                for b in range(B if product else 0):
                    product(pe, b).then_inc(made, 1)
                for b in range(B):
                    pe.wait_ge(squared, b + 1)
                    nc.tensor.matmul(g.ps[:, B + b, :], g.c("mean"), sq[:, b, :], start=True, stop=True)\
                        .then_inc(averaged, 1)

            @block.scalar
            def _(act):
                for b in range(B):
                    if product:
                        act.wait_ge(copied, b + 1)
                    nc.scalar.activation(sq[:, b, :], y[:, b, :], ACT.Square).then_inc(squared, 1)
                for b in range(B):
                    act.wait_ge(averaged, b + 1)
                    nc.scalar.activation(sq[:, b, :], g.ps[:, B + b, :], ACT.Ln, bias=g.eps[:, :])\
                        .then_inc(logged, 1)
                for b in range(B):
                    act.wait_ge(logged, b + 1)
                    nc.scalar.activation(sq[:, b, :], sq[:, b, :], ACT.Exp, scale=-0.5).then_inc(rooted, 1)

            @block.vector
            def _(dve):
                for b in range(B if product else 0):
                    dve.wait_ge(made, b + 1)
                    nc.vector.tensor_copy(y[:, b, :], g.ps[:, b, :]).then_inc(copied, 1)
                for b in range(B):
                    dve.wait_ge(rooted, b + 1)
                    nc.vector.scalar_tensor_tensor(out=y[:, b, :], in0=y[:, b, :], scalar=g.v(weight),
                                                   in1=sq[:, b, :], op0=ALU.mult, op1=ALU.mult).then_inc(scaled, 1)
                for b in range(B):
                    dve.wait_ge(scaled, b + 1)
                    nc.vector.tensor_tensor(out(b), y[:, b, :], base(b), ALU.add).then_inc(added, 1)


def ffn_attention(nc, g, xn, h):
    attention_stage(nc, g, "da", xn, g.w("fq"), g.w("fk"), g.w("fv"), 2, HD ** -0.5, h, causal=True)
    rms_add_stage(nc, g, "dr", lambda pe, b: nc.tensor.matmul(g.ps[:, b, :], g.w("fo"), h[:, b, :],
                                                              start=True, stop=True),
                  "attn_norm_w", lambda b: xn[:, b, :], lambda b: h[:, b, :])


def moe_gates(nc, g, xn, gates_dram, gates_ready):
    NTILE = NT // 128
    with ExitStack() as ctx:
        sem = ctx.enter_context(semaphores(nc, "mo"))

        def sb(name, shape):
            return ctx.enter_context(nc.sbuf_tensor(f"mo_{name}", shape, fp32))
        p, hot1, hot2, rank = (sb(n, [128, NTILE, E]) for n in ("p", "hot1", "hot2", "rank"))
        most = sb("most", [128, NTILE])
        gT = sb("gT", [E, B, T])
        routed, exped, lowered, step, turned, gT_ready = (
            sem(n) for n in ("routed", "exped", "lowered", "step", "turned", "gT_ready"))
        logits = g.ps[:, 4, 0:NTILE * E].rearrange("p (n e) -> p n e", e=E)
        spread = most[:, :].unsqueeze(2).broadcast_to([128, NTILE, E])
        order = g.c("order").unsqueeze(1).broadcast_to([128, NTILE, E])
        with nc.Block() as block:
            @block.tensor
            def _(pe):
                pe.wait_ge(g.weights_loaded[3], 16)
                for n in range(NTILE):
                    last = nc.tensor.matmul(logits[:, n, :], xn[:, n // QT, bass.ts(n % QT, 128)], g.w("router"),
                                            start=True, stop=True)
                last.then_inc(routed, 1)
                pe.wait_ge(step, 15)
                for n in range(NTILE):
                    last = nc.tensor.transpose(g.ps[0:E, n // QT, bass.ts(n % QT, 128)], p[:, n, :], g.c("ident"))
                last.then_inc(turned, 1)

            @block.scalar
            def _(act):
                act.wait_ge(lowered, 1)
                nc.scalar.activation(p[:, :, :], p[:, :, :], ACT.Exp).then_inc(exped, 1)
                act.wait_ge(turned, 1)
                for b in range(B):
                    nc.scalar.activation(gT[:, b, :], g.ps[0:E, b, :], ACT.Identity).then_inc(gT_ready, 1)

            @block.vector
            def _(dve):
                count = [0]

                def then(ins):
                    count[0] += 1
                    ins.then_inc(step, 1)
                    dve.wait_ge(step, count[0])
                dve.wait_ge(routed, 1)
                then(nc.vector.tensor_reduce(most[:, :], logits, AX.X, ALU.max, negate=True))
                nc.vector.tensor_tensor(p[:, :, :], logits, spread, ALU.add).then_inc(lowered, 1)
                dve.wait_ge(exped, 1)
                then(nc.vector.tensor_reduce(most[:, :], p[:, :, :], AX.X, ALU.add))
                then(nc.vector.reciprocal(most[:, :], most[:, :]))
                then(nc.vector.tensor_tensor(p[:, :, :], p[:, :, :], spread, ALU.mult))
                rest = p
                for hot in (hot1, hot2):
                    then(nc.vector.tensor_reduce(most[:, :], rest[:, :, :], AX.X, ALU.max))
                    then(nc.vector.tensor_tensor(rank[:, :, :], rest[:, :, :], spread, ALU.is_equal))
                    then(nc.vector.tensor_tensor(rank[:, :, :], rank[:, :, :], order, ALU.mult))
                    then(nc.vector.tensor_reduce(most[:, :], rank[:, :, :], AX.X, ALU.max))
                    then(nc.vector.tensor_tensor(hot[:, :, :], rank[:, :, :], spread, ALU.is_equal))
                    if hot is hot1:
                        nc.vector.scalar_tensor_tensor(out=hot2[:, :, :], in0=hot1[:, :, :], scalar=-2.0,
                                                       in1=p[:, :, :], op0=ALU.mult, op1=ALU.add)\
                            .then_inc(lowered, 1)
                        dve.wait_ge(lowered, 2)
                        rest = hot2
                nc.vector.tensor_tensor(hot1[:, :, :], hot1[:, :, :], hot2[:, :, :], ALU.add).then_inc(lowered, 1)
                dve.wait_ge(lowered, 3)
                then(nc.vector.tensor_tensor(p[:, :, :], p[:, :, :], hot1[:, :, :], ALU.mult))

            @block.sync
            def _(sp):
                sp.wait_ge(gT_ready, B)
                sp.dma_start(gates_dram, gT[:, :, :]).then_inc(gates_ready, 16)
                sp.wait_ge(gates_ready, 16)


def experts_stage(nc, g, xn, h, yd, ym, gates_dram):
    BLOCKS = [("dense", f) for f in range(FF // 128)] + [("expert", e) for e in range(E)]
    NB = len(BLOCKS)
    ND = FF // 128
    with ExitStack() as ctx:
        sem = ctx.enter_context(semaphores(nc, "ex"))

        def sb(name, shape):
            return ctx.enter_context(nc.sbuf_tensor(f"ex_{name}", shape, fp32))
        gates = sb("gates", [128, 2, E, T])
        s = sb("s", [128, 2, T])
        u = sb("u", [128, 3, T])
        up, activated, gated, weighted, dense_done, expert_done, out_copied = (
            sem(n) for n in ("up", "activated", "gated", "weighted", "dense_done", "expert_done", "out_copied"))
        down = sem("down")
        gates_loaded = [sem(f"gates_loaded_{n}") for n in range(2)]
        with nc.Block() as block:
            @block.sync
            def _(sp):
                for b in range(B):
                    if b >= 2:
                        sp.wait_ge(weighted, E * (b - 1))
                    sp.dma_start(gates[:, b % 2, :, :], gates_dram[:, b, :].partition_broadcast(128))\
                        .then_inc(gates_loaded[b % 2], 16)

            @block.tensor
            def _(pe):
                pe.wait_ge(g.weights_loaded[4], 16)

                def go_down(n):
                    b, i = divmod(n, NB)
                    kind, f = BLOCKS[i]
                    if kind == "dense":
                        pe.wait_ge(gated, n + 1)
                        w, bank, first, last_f = g.w("w2")[:, bass.ts(f, D)], 4 + b % 2, 0, ND - 1
                    else:
                        pe.wait_ge(weighted, E * b + f + 1)
                        w, bank, first, last_f = g.w("ew2")[:, bass.ts(f, D)], 6 + b % 2, 0, E - 1
                    if f == 0 and b >= 2:
                        pe.wait_ge(out_copied, 2 * (b - 1))
                    nc.tensor.matmul(g.ps[:, bank, :], w, u[:, n % 3, :], start=f == first, stop=f == last_f)\
                        .then_inc(down, 1)
                for n in range(B * NB):
                    b, i = divmod(n, NB)
                    kind, f = BLOCKS[i]
                    x, w1, w3 = (h, "w1", "w3") if kind == "dense" else (xn, "ew1", "ew3")
                    for m, w in enumerate((w1, w3)):
                        if n >= 2:
                            pe.wait_ge(activated if m == 0 else gated, n - 1)
                        last = nc.tensor.matmul(g.ps[:, 2 * m + n % 2, :], g.w(w)[:, bass.ts(f, 128)], x[:, b, :],
                                                start=True, stop=True).then_inc(up, 1)
                    if n >= 2:
                        go_down(n - 2)
                go_down(B * NB - 2)
                go_down(B * NB - 1)

            @block.scalar
            def _(act):
                for n in range(B * NB):
                    act.wait_ge(up, 2 * n + 1)
                    if n >= 2:
                        act.wait_ge(gated, n - 1)
                    nc.scalar.activation(s[:, n % 2, :], g.ps[:, n % 2, :], ACT.Silu).then_inc(activated, 1)

            @block.vector
            def _(dve):
                def copy_out(b):
                    dve.wait_ge(down, NB * b + ND)
                    nc.vector.tensor_copy(yd[:, b, :], g.ps[:, 4 + b % 2, :]).then_inc(out_copied, 1)
                    dve.wait_ge(down, NB * (b + 1))
                    nc.vector.tensor_copy(ym[:, b, :], g.ps[:, 6 + b % 2, :]).then_inc(out_copied, 1)
                for n in range(B * NB):
                    dve.wait_ge(up, 2 * n + 2)
                    dve.wait_ge(activated, n + 1)
                    if n >= 3:
                        dve.wait_ge(down, n - 2)
                    nc.vector.tensor_tensor(u[:, n % 3, :], g.ps[:, 2 + n % 2, :], s[:, n % 2, :], ALU.mult)\
                        .then_inc(gated, 1)
                    if n % NB == 4 and n > NB:
                        copy_out(n // NB - 1)
                copy_out(B - 1)

            @block.gpsimd
            def _(pool):
                for b in range(B):
                    pool.wait_ge(gates_loaded[b % 2], 16 * (b // 2 + 1))
                    for e in range(E):
                        n = NB * b + ND + e
                        pool.wait_ge(gated, n + 1)
                        nc.gpsimd.tensor_tensor(u[:, n % 3, :], u[:, n % 3, :], gates[:, b % 2, e, :], ALU.mult)\
                            .then_inc(weighted, 1)


def ffn_stage(nc, g):
    with ExitStack() as ctx:
        xn = ctx.enter_context(nc.sbuf_tensor("ff_xn", [D, B, T], fp32))
        norm_stage(nc, g, "ffln", lambda b: g.x[:, bass.ts(b, T)], lambda b: xn[:, b, :], "center", "mean")
        h = ctx.enter_context(nc.sbuf_tensor("ff_h", [D, B, T], fp32))
        ffn_attention(nc, g, xn, h)
        gates_dram = nc.dram_tensor("gates_scratch", [E, B, T], fp32, kind="Internal").ap()
        sem = ctx.enter_context(semaphores(nc, "ff"))
        gates_ready = sem("gates_ready")
        moe_gates(nc, g, xn, gates_dram, gates_ready)
        yd, ym = (ctx.enter_context(nc.sbuf_tensor(n, [D, B, T], fp32)) for n in ("ff_yd", "ff_ym"))
        experts_stage(nc, g, xn, h, yd, ym, gates_dram)
        rms_add_stage(nc, g, "rd", None, "ff_norm_w", lambda b: h[:, b, :], lambda b: h[:, b, :], y=yd)
        rms_add_stage(nc, g, "rm", None, "moe_norm_w", lambda b: h[:, b, :], lambda b: h[:, b, :], y=ym)
        added = sem("added")
        with nc.Block() as block:
            @block.vector
            def _(dve):
                for b in range(B):
                    nc.vector.tensor_tensor(g.x[:, bass.ts(b, T)], h[:, b, :], g.x[:, bass.ts(b, T)], ALU.add)\
                        .then_inc(added, 1)


def latent_stage(nc, g):
    NTILE = NT // 128
    NCH = XH * XD // 128
    with ExitStack() as ctx:
        sem = ctx.enter_context(semaphores(nc, "la"))

        def sb(name, shape):
            return ctx.enter_context(nc.sbuf_tensor(f"la_{name}", shape, fp32))
        lat = sb("lat", [D, B, T])
        cn = sb("cn", [D, B * LC])
        norm_stage(nc, g, "laln", lambda b: g.x[:, bass.ts(b, T)], lambda b: lat[:, b, :], "center", "mean")
        norm_stage(nc, g, "lcln", lambda b: g.ctxT[:, :], lambda b: cn[:, :], "center", "mean", chunks=1,
                   width=B * LC)
        kT, vT = (sb(n, [128, NCH, B * LC]) for n in ("kT", "vT"))
        A = sb("A", [D, XH, B * LC])
        U = sb("U", [128, B, XH // 4, D])
        p = sb("p", [128, 2, XH, LC])
        total = sb("total", [128, 2, XH])
        pT = sb("pT", [128, 2, XH // 4, T])
        (affined, k_made, k_copied, v_made, v_copied, a_made, a_copied, u_made, u_copied, scored, clipped, floored,
         exped, totalled, inverted, normed, turned, pT_copied, made, added) = (sem(n) for n in (
             "affined", "k_made", "k_copied", "v_made", "v_copied", "a_made", "a_copied", "u_made", "u_copied",
             "scored", "clipped", "floored", "exped", "totalled", "inverted", "normed", "turned", "pT_copied",
             "made", "added"))
        with nc.Block() as block:
            @block.tensor
            def _(pe):
                pe.wait_ge(g.weights_loaded[6], 16)
                pe.wait_ge(affined, 1)
                for side, made_ in ((0, k_made), (1, v_made)):
                    for c in range(NCH):
                        w = g.w("lkv")[:, side * XH * XD + c * 128:side * XH * XD + (c + 1) * 128]
                        last = nc.tensor.matmul(g.ps[:, 2 * side + c // 4, bass.ts(c % 4, 128)], w, cn[:, :],
                                                start=True, stop=True)
                        if c % 4 == 3:
                            last.then_inc(made_, 1)
                pe.wait_ge(k_copied, 2)
                for n in range(XH):
                    h = 2 * (n % 8) + n // 8
                    rows = slice(XD * (h % 2), XD * (h % 2) + XD)
                    last = nc.tensor.matmul(g.ps[:, 4 + n // 4, bass.ts(n % 4, 128)],
                                            g.w("lq").rearrange("p (c n) -> p c n", n=D)[rows, h // 2, :],
                                            kT[rows, h // 2, :], start=True, stop=True)
                    if n % 4 == 3:
                        last.then_inc(a_made, 1)
                pe.wait_ge(v_copied, 2)
                for b in range(B):
                    for h in range(XH):
                        rows = slice(XD * (h % 2), XD * (h % 2) + XD)
                        last = nc.tensor.matmul(g.ps[32 * (h % 4):32 * (h % 4) + LC, b, bass.ts(h // 4, D)],
                                                vT[rows, h // 2, bass.ts(b, LC)],
                                                g.w("lo").rearrange("p (c n) -> p c n", n=D)[rows, h // 2, :],
                                                start=True, stop=True)
                    last.then_inc(u_made, 1)

            @block.scalar
            def _(act):
                for n in range(2):
                    act.wait_ge(k_made, n + 1)
                    nc.scalar.activation(kT[:, 4 * n:4 * n + 4, :].rearrange("p c n -> p (c n)"), g.ps[:, n, :],
                                         ACT.Identity).then_inc(k_copied, 1)
                for n in range(4):
                    act.wait_ge(a_made, n + 1)
                    of_parity = A[:, :, :].rearrange("p (i two) n -> p two i n", two=2)[:, n // 2, :, :]
                    nc.scalar.activation(of_parity[:, 4 * (n % 2):4 * (n % 2) + 4, :],
                                         g.ps[:, 4 + n, :].rearrange("p (i n) -> p i n", n=128), ACT.Identity)\
                        .then_inc(a_copied, 1)

            @block.vector
            def _(dve):
                nc.vector.tensor_scalar(cn[:, :], cn[:, :], g.v("ln_c_w"), g.v("ln_c_b"), ALU.mult, ALU.add)\
                    .then_inc(affined, 1)
                for b in range(B):
                    nc.vector.tensor_scalar(lat[:, b, :], lat[:, b, :], g.v("ln_l_w"), g.v("ln_l_b"),
                                            ALU.mult, ALU.add).then_inc(affined, 1)
                for n in range(2):
                    dve.wait_ge(v_made, n + 1)
                    nc.vector.tensor_copy(vT[:, 4 * n:4 * n + 4, :].rearrange("p c n -> p (c n)"), g.ps[:, 2 + n, :])\
                        .then_inc(v_copied, 1)
                for b in range(B):
                    dve.wait_ge(u_made, b + 1)
                    nc.vector.tensor_copy(U[:, b, :, :].rearrange("p g n -> p (g n)"), g.ps[:, b, :])\
                        .then_inc(u_copied, 1)
        with nc.Block() as block:
            @block.tensor
            def _(pe):
                def turn(n):
                    pe.wait_ge(normed, n + 1)
                    if n >= 2:
                        pe.wait_ge(pT_copied, n - 1)
                    for grp in range(4):
                        last = nc.tensor.transpose(g.ps[:, 2 + n % 2, bass.ts(grp, 128)],
                                                   p[:, n % 2, 4 * grp:4 * grp + 4, :].rearrange("p h k -> p (h k)"),
                                                   g.c("ident"))
                    last.then_inc(turned, 1)

                def output(b):
                    pe.wait_ge(pT_copied, QT * (b + 1))
                    if b >= 2:
                        pe.wait_ge(added, b - 1)
                    for grp in range(4):
                        last = nc.tensor.matmul(g.ps[:, 4 + b % 2, :], U[:, b, grp, :], pT[:, b % 2, grp, :],
                                                start=grp == 0, stop=grp == 3)
                    last.then_inc(made, 1)
                for n in range(NTILE):
                    b, t = divmod(n, QT)
                    if n >= 2:
                        pe.wait_ge(clipped, n - 1)
                    nc.tensor.matmul(g.ps[:, n % 2, :].rearrange("p (h k) -> p h k", k=LC),
                                     lat[:, b, bass.ts(t, 128)], A[:, :, bass.ts(b, LC)], start=True, stop=True)\
                        .then_inc(scored, 1)
                    if n >= 1:
                        turn(n - 1)
                    if n >= QT and t == 1:
                        output(b - 1)
                turn(NTILE - 1)
                output(B - 1)

            @block.vector
            def _(dve):
                def average(n):
                    dve.wait_ge(exped, n + 1)
                    nc.vector.tensor_reduce(total[:, n % 2, :], p[:, n % 2, :, :], AX.X, ALU.add).then_inc(totalled, 1)
                    dve.wait_ge(totalled, n + 1)
                    nc.vector.reciprocal(total[:, n % 2, :], total[:, n % 2, :]).then_inc(inverted, 1)

                def add(b):
                    dve.wait_ge(made, b + 1)
                    nc.vector.scalar_tensor_tensor(out=g.x[:, bass.ts(b, T)], in0=g.ps[:, 4 + b % 2, :],
                                                   scalar=g.v("bo"), in1=g.x[:, bass.ts(b, T)],
                                                   op0=ALU.add, op1=ALU.add).then_inc(added, 1)
                for n in range(NTILE):
                    dve.wait_ge(scored, n + 1)
                    if n >= 2:
                        dve.wait_ge(turned, n - 1)
                    nc.vector.tensor_scalar(p[:, n % 2, :, :].rearrange("p h k -> p (h k)"), g.ps[:, n % 2, :],
                                            XD ** -0.5, 11.0, ALU.mult, ALU.min).then_inc(clipped, 1)
                    dve.wait_ge(clipped, n + 1)
                    flat = p[:, n % 2, :, :].rearrange("p h k -> p (h k)")
                    nc.vector.tensor_scalar(flat, flat, -11.0, None, ALU.max).then_inc(floored, 1)
                    average(n)
                    if n >= QT and n % QT == 2:
                        add(n // QT - 1)
                add(B - 1)

            @block.gpsimd
            def _(pool):
                for n in range(NTILE):
                    pool.wait_ge(inverted, n + 1)
                    nc.gpsimd.tensor_tensor(p[:, n % 2, :, :], p[:, n % 2, :, :],
                                            total[:, n % 2, :].unsqueeze(2).broadcast_to([128, XH, LC]), ALU.mult)\
                        .then_inc(normed, 1)

            @block.scalar
            def _(act):
                def copy(n):
                    b, t = divmod(n, QT)
                    act.wait_ge(turned, n + 1)
                    if b >= 2 and t == 0:
                        act.wait_ge(made, b - 1)
                    nc.scalar.activation(pT[:, b % 2, :, bass.ts(t, 128)],
                                         g.ps[:, 2 + n % 2, :].rearrange("p (g q) -> p g q", q=128), ACT.Identity)\
                        .then_inc(pT_copied, 1)
                for n in range(NTILE):
                    act.wait_ge(floored, n + 1)
                    flat = p[:, n % 2, :, :].rearrange("p h k -> p (h k)")
                    nc.scalar.activation(flat, flat, ACT.Exp).then_inc(exped, 1)
                    if n >= 1:
                        copy(n - 1)
                copy(NTILE - 1)



QG = 8
TILES = T // QG


def relative_stage(nc, g, ins):
    WIN = 2 * REL + QG
    NTILES = B * TILES
    GT = 128 // QG
    GROUPS = B * QT
    with ExitStack() as ctx:
        sem = ctx.enter_context(semaphores(nc, "re"))

        def sb(name, shape, dt=fp32):
            return ctx.enter_context(nc.sbuf_tensor(f"re_{name}", shape, dt))
        o_dram = nc.dram_tensor("re_o_scratch", [B, TILES, 128, HD], fp32, kind="Internal").ap()
        osum_dram = nc.dram_tensor("re_osum_scratch", [B, QT, 128, H // 4, 128], fp32, kind="Internal").ap()
        q_dram = nc.dram_tensor("re_q_scratch", [NT, D], fp32, kind="Internal").ap()
        with ExitStack() as inner:
            def isb(name, shape, dt=fp32):
                return inner.enter_context(nc.sbuf_tensor(f"re_{name}", shape, dt))
            q, k = isb("q", [D, B, T]), isb("k", [D, B, T])
            v9 = isb("v9", [128, B * QT, H, HD + 1])
            rel_k = isb("rel_k", [128, WIN])
            rel_v = isb("rel_v", [128, 256, HD])
            ends = isb("ends", [128, 2, HD + 1])
            qrel = isb("qrel", [128, 2, QG, H])
            with ExitStack() as proj:
                xn = proj.enter_context(nc.sbuf_tensor("re_xn", [D, B, T], fp32))
                bq = proj.enter_context(nc.sbuf_tensor("re_bq", [D, 1], fp32))
                q_tok = proj.enter_context(nc.sbuf_tensor("re_q_tok", [128, B, QT, D], fp32))
                norm_stage(nc, g, "reln", lambda b: g.x[:, bass.ts(b, T)], lambda b: xn[:, b, :], "center", "mean")
                k_table, v_table, ends_loaded, q_stored, set_up, cut_off, less = (
                    sem(n) for n in ("k_table", "v_table", "ends_loaded", "q_stored", "set_up", "cut_off", "less"))
                projected, copied, scaled_bias, swapped, q_out = (
                    sem(n) for n in ("projected", "copied", "scaled_bias", "swapped", "q_out"))
                with nc.Block() as block:
                    @block.sync
                    def _(sp):
                        for c in range(QG):
                            at = QG - 1 - c + T - REL
                            sp.dma_start(rel_k[c * HD:(c + 1) * HD, :], ins["rel_k"][:, at:at + WIN])\
                                .then_inc(k_table, 16)
                        src = ins["rel_v"]
                        for to, n, at in ((0, 128, T - 128), (128, 64, T - 256 + 64), (192, 64, T)):
                            overlapping = bass.AP(src.tensor, at * HD, [[HD, 128], [1, n * HD]])
                            sp.dma_start(rel_v[:, to:to + n, :].rearrange("p s d -> p (s d)"), overlapping)\
                                .then_inc(v_table, 16)
                        sp.wait_ge(set_up, 1)
                        for n, row in ((0, 0), (1, src.shape[0] - 1)):
                            one_row = bass.AP(src.tensor, row * HD, [[0, 128], [1, HD]])
                            sp.dma_start(ends[:, n, 0:HD], one_row).then_inc(ends_loaded, 16)
                        for b in range(B):
                            sp.wait_ge(q_out, b + 1)
                            sp.dma_start(q_dram[b * T:(b + 1) * T, :].rearrange("(t p) c -> p t c", p=128),
                                         q_tok[:, b, :, :]).then_inc(q_stored, 16)
                        sp.wait_ge(q_stored, 16 * B)

                    @block.gpsimd
                    def _(pool):
                        nc.gpsimd.memset(ends[:, :, :], 0.0).then_inc(set_up, 1)
                        nc.gpsimd.memset(v9[:, :, :, HD:HD + 1], 1.0).then_inc(set_up, 1)

                    @block.tensor
                    def _(pe):
                        pe.wait_ge(g.weights_loaded[5], 16)
                        for n in range(3 * B):
                            b, s = divmod(n, 3)
                            if n >= 8:
                                pe.wait_ge(copied, n - 7)
                            w = g.w("aqkv")[:, s * D:(s + 1) * D]
                            if s < 2:
                                nc.tensor.matmul(g.ps[:, n % 8, :], w, xn[:, b, :], start=True, stop=True)\
                                    .then_inc(projected, 1)
                            else:
                                for t in range(QT):
                                    last = nc.tensor.matmul(g.ps[:, n % 8, bass.ts(t, 128)],
                                                            xn[:, b, bass.ts(t, 128)], w, start=True, stop=True)
                                last.then_inc(projected, 1)
                        for b in range(B):
                            pe.wait_ge(copied, max(3 * b + 1, 5 + b))
                            for t in range(QT):
                                last = nc.tensor.matmul(g.ps[:, 4 + b, bass.ts(t, 128)], q[:, b, bass.ts(t, 128)],
                                                        g.c("to_dh"), start=True, stop=True)
                            last.then_inc(swapped, 1)

                    @block.scalar
                    def _(act):
                        nc.scalar.activation(bq[:, :], g.v("b_q"), ACT.Identity, scale=HD ** -0.5)\
                            .then_inc(scaled_bias, 1)
                        act.wait_ge(scaled_bias, 1)
                        for n in range(3 * B):
                            b, s = divmod(n, 3)
                            act.wait_ge(projected, n + 1)
                            if s == 0:
                                nc.scalar.activation(q[:, b, :], g.ps[:, n % 8, :], ACT.Identity, bias=bq[:, :],
                                                     scale=HD ** -0.5).then_inc(copied, 1)
                            elif s == 1:
                                nc.scalar.activation(k[:, b, :], g.ps[:, n % 8, :], ACT.Identity, bias=g.v("b_k"))\
                                    .then_inc(copied, 1)
                            else:
                                nc.scalar.activation(
                                    v9[:, QT * b:QT * b + QT, :, 0:HD],
                                    g.ps[:, n % 8, :].rearrange("p (t h d) -> p t h d", t=QT, d=HD), ACT.Identity)\
                                    .then_inc(copied, 1)

                    @block.vector
                    def _(dve):
                        nc.vector.memset(rel_k[64:128, :], 0.0).then_inc(cut_off, 1)
                        nc.vector.memset(qrel[64:128, :, :, :], 0.0).then_inc(cut_off, 1)
                        dve.wait_ge(k_table, 16 * QG)
                        low, high = rel_k[0:64, 0:REL], rel_k[0:64, REL:WIN]
                        nc.vector.tensor_scalar(low, low, g.v("rel_k_lo")[0:64, :], None, ALU.subtract)\
                            .then_inc(less, 1)
                        nc.vector.tensor_scalar(high, high, g.v("rel_k_hi")[0:64, :], None, ALU.subtract)\
                            .then_inc(less, 1)
                        dve.wait_ge(v_table, 48)
                        dve.wait_ge(ends_loaded, 32)
                        for n in range(2):
                            part = rel_v[:, 128 + 64 * n:192 + 64 * n, :]
                            nc.vector.tensor_tensor(part, part, ends[:, n:n + 1, 0:HD].broadcast_to([128, 64, HD]),
                                                    ALU.subtract).then_inc(less, 1)
                        for b in range(B):
                            dve.wait_ge(swapped, b + 1)
                            nc.vector.tensor_copy(q_tok[:, b, :, :].rearrange("p t c -> p (t c)"), g.ps[:, 4 + b, :])\
                                .then_inc(q_out, 1)
            qd = isb("qd", [QG * HD, 2, TILES, H])
            keys = isb("keys", [D, 2, 2, T])
            qbd = isb("qbd", [D, 2, QG, H])
            v_far = isb("v_far", [128, 2, 2, QT, H, HD + 1])
            nmax, total, inv = (isb(n, [128, 2]) for n in ("nmax", "total", "inv"))
            p = isb("p", [128, 2, T])
            pT = isb("pT", [128, 2, QT, GT, 128])
            picked = isb("picked", [128, 2, 2, HD])
            o = isb("o", [128, 2, TILES, HD])
            osum = isb("osum", [128, 2, H // 4, 128])
            zero = isb("zero", [128, 128])
            (zeroed, cleared, qd_loaded, keys_set, keys_moved, qbd_ready, qrel_ready, far_ready, scored, maxed,
             exped, turned, pT_ready, near_done, value_step, inverted, masked, o_done, osum_out) = (
                 sem(n) for n in ("zeroed", "cleared", "qd_loaded", "keys_set", "keys_moved", "qbd_ready",
                                  "qrel_ready", "far_ready", "scored", "maxed", "exped", "turned", "pT_ready",
                                  "near_done", "value_step", "inverted", "masked", "o_done", "osum_out"))
            o_stored, osum_stored = sem("o_stored"), [sem(f"osum_stored_{n}") for n in range(2)]
            S_BANK, T_BANK, V_BANK, N_BANK = 0, 2, 4, 6
            LAG = GT + 2
            with nc.Block() as block:
                @block.gpsimd
                def _(pool):
                    nc.gpsimd.memset(zero[:, :], 0.0).then_inc(zeroed, 1)

                    def set_keys(b):
                        for m in range(2):
                            nc.gpsimd.tensor_tensor(keys[:, b % 2, m, :], k[:, b, :],
                                                    g.v("rel_k_hi").broadcast_to([D, T]), ALU.add).then_inc(keys_set, 1)

                    def far_values(b):
                        for n in range(2):
                            nc.gpsimd.tensor_tensor(
                                v_far[:, b % 2, n, :, :, :].rearrange("p t h d -> p (t h) d"),
                                v9[:, QT * b:QT * b + QT, :, :].rearrange("p t h d -> p (t h) d"),
                                ends[:, n:n + 1, :].broadcast_to([128, QT * H, HD + 1]), ALU.add)\
                                .then_inc(far_ready, 1)
                    set_keys(0)
                    far_values(0)
                    for i in range(NTILES):
                        b, a = divmod(i, TILES)
                        m = i % 2
                        if i >= 2:
                            pool.wait_ge(scored, i - 1)
                        if a >= 1:
                            seen = slice(QG * max(a - 2, 0), QG * a)
                            pool.wait_ge(keys_set, 2 * (b + 1))
                            if b * (TILES - 1) + a > 1:
                                pool.wait_ge(keys_moved, b * (TILES - 1) + a - 1)
                            nc.gpsimd.tensor_tensor(keys[:, b % 2, m, seen], k[:, b, seen],
                                                    g.v("rel_k_lo").broadcast_to([D, seen.stop - seen.start]),
                                                    ALU.add).then_inc(keys_moved, 1)
                        at = QG * a
                        nc.gpsimd.tensor_tensor(qbd[:, m, :, :], q[:, b, at:at + QG].unsqueeze(2)
                                                .broadcast_to([D, QG, H]),
                                                g.c("headmask").unsqueeze(1).broadcast_to([D, QG, H]), ALU.mult)\
                            .then_inc(qbd_ready, 1)
                        if a == 0:
                            pool.wait_ge(qd_loaded, 16 * (b + 1))
                        nc.gpsimd.tensor_tensor(qrel[0:QG * HD, m, :, :],
                                                qd[:, b % 2, a:a + 1, :].broadcast_to([QG * HD, QG, H]),
                                                g.c("own_c")[0:QG * HD, :].rearrange("p (c h) -> p c h", h=H),
                                                ALU.mult).then_inc(qrel_ready, 1)
                        if a == TILES // 2 and b + 1 < B:
                            set_keys(b + 1)
                            if b >= 1:
                                pool.wait_ge(value_step, GT * QT * b)
                            far_values(b + 1)

                @block.tensor
                def _(pe):
                    def score(i):
                        b, a = divmod(i, TILES)
                        m = i % 2
                        pe.wait_ge(keys_set, 2 * b + m + 1)
                        if b * (TILES - 1) + a >= 1:
                            pe.wait_ge(keys_moved, b * (TILES - 1) + a)
                        pe.wait_ge(qbd_ready, i + 1)
                        pe.wait_ge(qrel_ready, i + 1)
                        if i >= 2:
                            pe.wait_ge(exped, i - 1)
                        nc.tensor.matmul(g.ps[:, S_BANK + m, :], qbd[:, m, :, :].rearrange("p c h -> p (c h)"),
                                         keys[:, b % 2, m, :], start=True, stop=False)
                        first = QG * a - REL
                        lo, hi = max(first, 0), min(first + WIN, T)
                        nc.tensor.matmul(g.ps[:, S_BANK + m, lo:hi], qrel[:, m, :, :].rearrange("p c h -> p (c h)"),
                                         rel_k[:, lo - first:hi - first], start=False, stop=True)\
                            .then_inc(scored, 1)

                    def turn(i):
                        m = i % 2
                        pe.wait_ge(exped, i + 1)
                        if i >= 2:
                            pe.wait_ge(pT_ready, i - 1)
                        for kt in range(QT):
                            last = nc.tensor.transpose(g.ps[:, T_BANK + m, bass.ts(kt, 128)],
                                                       p[:, m, bass.ts(kt, 128)], g.c("ident"))
                        last.then_inc(turned, 1)

                    def near_values(i):
                        m = i % 2
                        n, a = divmod(i, GT)
                        qt = n % QT
                        pe.wait_ge(pT_ready, i + 1)
                        if i >= 2:
                            pe.wait_ge(masked, i - 1)
                        tiles = [(qt, 0, 0)]
                        if a < GT // 2 and qt > 0:
                            tiles.append((qt - 1, 128, 64))
                        if a >= GT // 2 and qt < QT - 1:
                            tiles.append((qt + 1, 192, 0))
                        for kt, base, s0 in tiles:
                            for j in range(4):
                                s = 127 - (QG * a + 2 * j + 1) - s0 + base
                                last = nc.tensor.matmul(
                                    g.ps[32 * j:32 * j + 32, N_BANK + m, 0:2 * HD],
                                    pT[:, n % 2, kt, a, 32 * j:32 * j + 32],
                                    rel_v[:, s:s + 2, :].rearrange("p s d -> p (s d)"),
                                    start=kt == qt, stop=kt == tiles[-1][0])
                        last.then_inc(near_done, 1)

                    def far_step(i):
                        n, step = divmod(i, GT)
                        b, qt = divmod(n, QT)
                        quad, kt = divmod(step, QT)
                        if step == 0:
                            pe.wait_ge(pT_ready, GT * (n + 1))
                            pe.wait_ge(far_ready, 2 * (b + 1))
                            if n >= 2:
                                pe.wait_ge(osum_out, n - 1)
                        for j in range(4):
                            h = 4 * quad + j
                            if kt == qt:
                                values = v9[:, QT * b + kt, h, :]
                            else:
                                values = v_far[:, b % 2, int(kt > qt), kt, h, :]
                            weights = pT[:, n % 2, kt, :, :].rearrange("p a (c h) -> p (a c) h", h=H)[:, :, h]
                            last = nc.tensor.matmul(g.ps[32 * j:32 * j + HD + 1, V_BANK + n % 2, bass.ts(quad, 128)],
                                                    values, weights, start=kt == 0, stop=kt == QT - 1)
                        last.then_inc(value_step, 1)

                    pe.wait_ge(zeroed, 1)
                    for n in range(2):
                        for quad in range(4):
                            nc.tensor.matmul(g.ps[:, V_BANK + n, bass.ts(quad, 128)], zero[:, :], zero[:, :],
                                             start=True, stop=True).then_inc(cleared, 1)
                    for i in range(NTILES + LAG):
                        if i < NTILES:
                            score(i)
                        if 1 <= i <= NTILES:
                            turn(i - 1)
                        if 2 <= i <= NTILES + 1:
                            near_values(i - 2)
                        if i >= LAG:
                            far_step(i - LAG)

                @block.scalar
                def _(act):
                    def copy_sums(n):
                        act.wait_ge(value_step, GT * (n + 1))
                        if n >= 2:
                            act.wait_ge(osum_stored[n % 2], 16 * (n // 2))
                        nc.scalar.activation(osum[:, n % 2, :, :].rearrange("p g q -> p (g q)"),
                                             g.ps[:, V_BANK + n % 2, :], ACT.Identity).then_inc(osum_out, 1)
                    act.wait_ge(cleared, 8)
                    for i in range(NTILES + 1):
                        m = i % 2
                        if i < NTILES:
                            act.wait_ge(maxed, i + 1)
                            if i >= 2:
                                act.wait_ge(turned, i - 1)
                                act.wait_ge(inverted, i - 1)
                            nc.scalar.activation(p[:, m, :], g.ps[:, S_BANK + m, :], ACT.Exp, bias=nmax[:, m:m + 1],
                                                 accum_out=total[:, m:m + 1]).then_inc(exped, 1)
                        if i >= 1:
                            n, a = divmod(i - 1, GT)
                            act.wait_ge(turned, i)
                            if n >= 2 and a == 0:
                                act.wait_ge(value_step, GT * (n - 1))
                                act.wait_ge(near_done, GT * (n - 1))
                            nc.scalar.activation(pT[:, n % 2, :, a, :],
                                                 g.ps[:, T_BANK + 1 - m, :].rearrange("p (t c) -> p t c", c=128),
                                                 ACT.Identity).then_inc(pT_ready, 1)
                        if i >= LAG + GT and (i - LAG) % GT == 1:
                            copy_sums((i - LAG) // GT - 1)
                    copy_sums(GROUPS - 2)
                    copy_sums(GROUPS - 1)

                @block.vector
                def _(dve):
                    for i in range(NTILES + 2):
                        m = i % 2
                        if i < NTILES:
                            dve.wait_ge(scored, i + 1)
                            nc.vector.tensor_reduce(nmax[:, m:m + 1], g.ps[:, S_BANK + m, :], AX.X, ALU.max,
                                                    negate=True).then_inc(maxed, 1)
                        if 1 <= i <= NTILES:
                            dve.wait_ge(exped, i)
                            nc.vector.reciprocal(inv[:, 1 - m:2 - m], total[:, 1 - m:2 - m]).then_inc(inverted, 1)
                        if i >= 2:
                            b, a = divmod(i - 2, TILES)
                            dve.wait_ge(near_done, i - 1)
                            dve.wait_ge(inverted, i - 1)
                            nc.vector.scalar_tensor_tensor(
                                out=picked[:, m, :, :].rearrange("p s d -> p (s d)"),
                                in0=g.ps[:, N_BANK + m, 0:2 * HD], scalar=inv[:, m:m + 1],
                                in1=g.c("own_pair"), op0=ALU.mult, op1=ALU.mult).then_inc(masked, 1)
                            dve.wait_ge(masked, i - 1)
                            if b >= 2 and a == 0:
                                dve.wait_ge(o_stored, 16 * (b - 1))
                            nc.vector.tensor_tensor(o[:, b % 2, a, :], picked[:, m, 0, :], picked[:, m, 1, :],
                                                    ALU.add).then_inc(o_done, 1)

                @block.sync
                def _(sp):
                    def load_queries(b):
                        src = q_dram[b * T:(b + 1) * T, :].rearrange("(i c) (d h) -> (c d) i h", c=QG, h=H)
                        sp.dma_start(qd[:, b % 2, :, :], src).then_inc(qd_loaded, 16)
                        sp.wait_ge(qd_loaded, 16 * (b + 1))
                    load_queries(0)
                    load_queries(1)
                    for n in range(GROUPS):
                        b, qt = divmod(n, QT)
                        sp.wait_ge(osum_out, n + 1)
                        sp.dma_start(osum_dram[b, qt], osum[:, n % 2, :, :]).then_inc(osum_stored[n % 2], 16)
                        if qt == 0 and b >= 1:
                            sp.wait_ge(o_done, TILES * b)
                            if b >= 2:
                                sp.wait_ge(o_stored, 16 * (b - 1))
                            sp.dma_start(o_dram[b - 1].rearrange("a p d -> p a d"), o[:, (b - 1) % 2, :, :])\
                                .then_inc(o_stored, 16)
                            if b + 1 < B:
                                load_queries(b + 1)
                    sp.wait_ge(o_done, NTILES)
                    sp.wait_ge(o_stored, 16 * (B - 1))
                    sp.dma_start(o_dram[B - 1].rearrange("a p d -> p a d"), o[:, (B - 1) % 2, :, :])\
                        .then_inc(o_stored, 16)
                    sp.wait_ge(o_stored, 16 * B)
                    for n in range(2):
                        sp.wait_ge(osum_stored[n], 16 * (GROUPS // 2))
        osum_all = sb("osum_all", [128, B, H // 4, T])
        o_far = sb("o_far", [D, B, T])
        ot = sb("ot", [128, B * QT, D])
        oT = sb("oT", [D, B, T])
        loaded, sums_loaded, back, biased, made, added = (
            sem(n) for n in ("loaded", "sums_loaded", "back", "biased", "made", "added"))
        with nc.Block() as block:
            @block.sync
            def _(sp):
                rows = o_dram.rearrange("b a p d -> (b a p d)").rearrange("(n p c) -> p n c", p=128, c=D)
                sp.dma_start(ot[:, :, :], rows).then_inc(loaded, 16)
                for b in range(B):
                    sp.dma_start(osum_all[:, b, :, :].rearrange("p g (t n) -> p g t n", n=128),
                                 osum_dram[b].rearrange("t p g n -> p g t n")).then_inc(sums_loaded, 16)
                sp.wait_ge(sums_loaded, 16 * B)
        join_heads_stage(nc, g, "re", osum_all, o_far)
        with nc.Block() as block:
            @block.tensor
            def _(pe):
                pe.wait_ge(loaded, 16)
                for n in range(B * QT):
                    last = nc.tensor.transpose(g.ps[:, n // QT, bass.ts(n % QT, 128)], ot[:, n, :], g.c("ident"))
                    if n % QT == QT - 1:
                        last.then_inc(back, 1)
                for b in range(B):
                    nc.tensor.matmul(g.ps[:, 4 + b, :], g.w("aout"), o_far[:, b, :], start=True, stop=False)
                    pe.wait_ge(biased, b + 1)
                    nc.tensor.matmul(g.ps[:, 4 + b, :], g.w("aout"), oT[:, b, :], start=False, stop=True)\
                        .then_inc(made, 1)

            @block.scalar
            def _(act):
                for b in range(B):
                    act.wait_ge(back, b + 1)
                    nc.scalar.activation(oT[:, b, :], g.ps[:, b, :], ACT.Identity, bias=g.v("b_v")).then_inc(biased, 1)

            @block.vector
            def _(dve):
                for b in range(B):
                    dve.wait_ge(made, b + 1)
                    nc.vector.scalar_tensor_tensor(out=g.x[:, bass.ts(b, T)], in0=g.ps[:, 4 + b, :],
                                                   scalar=g.v("b_out"), in1=g.x[:, bass.ts(b, T)],
                                                   op0=ALU.add, op1=ALU.add).then_inc(added, 1)


def grouped_stage(nc, g):
    with ExitStack() as ctx:
        sem = ctx.enter_context(semaphores(nc, "gr"))

        def sb(name, shape, dt=fp32):
            return ctx.enter_context(nc.sbuf_tensor(f"gr_{name}", shape, dt))
        xn = sb("xn", [D, B, T])
        o = sb("o", [D, B, T])
        reg_o = sb("reg_o", [D, B, QG])
        norm_stage(nc, g, "grln", lambda b: g.x[:, bass.ts(b, T)], lambda b: xn[:, b, :], "center", "mean")
        rows_dram = nc.dram_tensor("gr_rows_scratch", [4, B, T], bf16, kind="Internal").ap()
        SCALE = HD ** -0.5
        with ExitStack() as inner:
            def isb(name, shape, dt=fp32):
                return inner.enter_context(nc.sbuf_tensor(f"gr_{name}", shape, dt))
            q, k = isb("q", [D, B, T]), isb("k", [D, B, T])
            v = isb("v", [128, B * QT, D])
            sq = isb("sq", [D, B, T])
            gsq, gn = isb("gsq", [D, 1]), isb("gn", [D, 1])
            guide = isb("guide", [D, 32])
            sim = isb("sim", [128, T])
            ends, ends_all = isb("ends", [128, 2]), isb("ends_all", [128, 2])
            span = isb("span", [128, 1])
            rows = isb("rows", [128, 4, T], bf16)
            lowered = isb("lowered", [1, B, T], bf16)
            (projected, squared, copied, normed2, logged, rooted, divided, g_squared, g_normed, g_logged, g_rooted,
             g_ready, compared, ended, gathered, step, rows_made, rows_stored, back) = (sem(n) for n in (
                 "projected", "squared", "copied", "normed2", "logged", "rooted", "divided", "g_squared",
                 "g_normed", "g_logged", "g_rooted", "g_ready", "compared", "ended", "gathered", "step",
                 "rows_made", "rows_stored", "back"))
            with nc.Block() as block:
                @block.tensor
                def _(pe):
                    pe.wait_ge(g.weights_loaded[7], 16)
                    for b in range(B):
                        nc.tensor.matmul(g.ps[:, b, :], g.w("gqkv")[:, 0:D], xn[:, b, :], start=True, stop=True)\
                            .then_inc(projected, 1)
                    for b in range(B):
                        pe.wait_ge(squared, b + 1)
                        nc.tensor.matmul(g.ps[:, 4 + b, :], g.c("hsum"), sq[:, b, :], start=True, stop=True)\
                            .then_inc(normed2, 1)
                    for b in range(B):
                        pe.wait_ge(copied, b + 1)
                        nc.tensor.matmul(g.ps[:, b, :], g.w("gqkv")[:, D:2 * D], xn[:, b, :], start=True, stop=True)\
                            .then_inc(projected, 1)
                    for b in range(B):
                        pe.wait_ge(logged, b + 1)
                        for t in range(QT):
                            last = nc.tensor.matmul(g.ps[:, 4 + b, bass.ts(t, 128)], xn[:, b, bass.ts(t, 128)],
                                                    g.w("gqkv")[:, 2 * D:3 * D], start=True, stop=True)
                        last.then_inc(projected, 1)
                    pe.wait_ge(g_squared, 1)
                    pe.wait_ge(copied, B + 1)
                    nc.tensor.matmul(g.ps[:, 0, 0:1], g.c("hsum"), gsq[:, :], start=True, stop=True)\
                        .then_inc(g_normed, 1)
                    pe.wait_ge(g_ready, 1)
                    pe.wait_ge(copied, B + 2)
                    for b in range(B):
                        pe.wait_ge(divided, b + 1)
                        last = nc.tensor.matmul(g.ps[32 * b:32 * b + 32, 1, :], guide[:, :], sq[:, b, :],
                                                start=True, stop=True)
                    last.then_inc(compared, 1)

                @block.scalar
                def _(act):
                    nc.scalar.activation(gsq[:, :], g.v("g_q"), ACT.Square).then_inc(g_squared, 1)
                    for b in range(B):
                        act.wait_ge(copied, b + 1)
                        nc.scalar.activation(sq[:, b, :], q[:, b, :], ACT.Square).then_inc(squared, 1)
                    for b in range(B):
                        act.wait_ge(normed2, b + 1)
                        nc.scalar.activation(sq[:, b, :], g.ps[:, 4 + b, :], ACT.Ln).then_inc(logged, 1)
                    act.wait_ge(g_normed, 1)
                    nc.scalar.activation(gn[:, :], g.ps[:, 0, 0:1], ACT.Ln).then_inc(g_logged, 1)
                    for b in range(B):
                        act.wait_ge(logged, b + 1)
                        nc.scalar.activation(sq[:, b, :], sq[:, b, :], ACT.Exp, scale=-0.5).then_inc(rooted, 1)
                    act.wait_ge(g_logged, 1)
                    nc.scalar.activation(gn[:, :], gn[:, :], ACT.Exp, scale=-0.5).then_inc(g_rooted, 1)

                @block.vector
                def _(dve):
                    for b in range(B):
                        dve.wait_ge(projected, b + 1)
                        nc.vector.tensor_copy(q[:, b, :], g.ps[:, b, :]).then_inc(copied, 1)
                    for b in range(B):
                        dve.wait_ge(projected, B + b + 1)
                        nc.vector.tensor_copy(k[:, b, :], g.ps[:, b, :]).then_inc(copied, 1)
                    for b in range(B):
                        dve.wait_ge(projected, 2 * B + b + 1)
                        nc.vector.tensor_copy(v[:, QT * b:QT * b + QT, :].rearrange("p t c -> p (t c)"),
                                              g.ps[:, 4 + b, :]).then_inc(back, 1)
                    dve.wait_ge(g_rooted, 1)
                    nc.vector.tensor_scalar(guide[:, :], g.v("g_q").broadcast_to([D, 32]), gn[:, :], 1.0 / H,
                                            ALU.mult, ALU.mult).then_inc(g_ready, 1)
                    for b in range(B):
                        dve.wait_ge(rooted, b + 1)
                        nc.vector.tensor_tensor(sq[:, b, :], sq[:, b, :], q[:, b, :], ALU.mult).then_inc(divided, 1)
                    dve.wait_ge(compared, 1)
                    nc.vector.tensor_copy(sim[:, :], g.ps[:, 1, :]).then_inc(ended, 1)
                    dve.wait_ge(ended, 1)
                    nc.vector.tensor_reduce(ends[:, 0:1], sim[:, REG:T], AX.X, ALU.min, negate=True).then_inc(ended, 1)
                    nc.vector.tensor_reduce(ends[:, 1:2], sim[:, REG:T], AX.X, ALU.max).then_inc(ended, 1)
                    dve.wait_ge(gathered, 1)
                    count = [0]

                    def then(ins):
                        count[0] += 1
                        ins.then_inc(step, 1)
                        dve.wait_ge(step, count[0])
                    then(nc.vector.tensor_tensor(span[:, :], ends_all[:, 0:1], ends_all[:, 1:2], ALU.add))
                    then(nc.vector.reciprocal(span[:, :], span[:, :]))
                    then(nc.vector.tensor_scalar(sim[:, :], sim[:, :], ends_all[:, 0:1], span[:, :],
                                                 ALU.add, ALU.mult))
                    then(nc.vector.tensor_single_scalar(sim[:, :], sim[:, :], 0.9, ALU.is_gt))
                    nc.vector.tensor_copy(rows[:, 0, :], sim[:, :]).then_inc(rows_made, 1)
                    nc.vector.tensor_scalar(rows[:, 1, :], sim[:, :], -1.0, 1.0, ALU.mult, ALU.add)\
                        .then_inc(rows_made, 1)
                    nc.vector.tensor_scalar(rows[:, 2, :], sim[:, :], -1.0, BIG, ALU.add, ALU.mult)\
                        .then_inc(rows_made, 1)
                    nc.vector.tensor_scalar(rows[:, 3, :], sim[:, :], -BIG, None, ALU.mult).then_inc(rows_made, 1)
                    dve.wait_ge(rows_made, 4)
                    nc.vector.memset(rows[:, 0, 0:REG], 1.0).then_inc(rows_made, 1)
                    nc.vector.memset(rows[:, 1:4, 0:REG], 0.0).then_inc(rows_made, 1)

                @block.gpsimd
                def _(pool):
                    pool.wait_ge(ended, 3)
                    nc.gpsimd.partition_all_reduce(ends_all[:, :], ends[:, :], 128, bass.bass_isa.ReduceOp.max)\
                        .then_inc(gathered, 1)

                @block.sync
                def _(sp):
                    sp.wait_ge(rows_made, 6)
                    for b in range(B):
                        sp.dma_start(rows_dram[:, b, :], rows[32 * b:32 * b + 1, :, :]).then_inc(rows_stored, 16)
                    sp.wait_ge(rows_stored, 16 * B)
                    sp.dma_start(lowered[:, :, :], rows_dram[3:4, :, :]).then_inc(rows_stored, 16)
                    sp.wait_ge(rows_stored, 16 * (B + 1))
            qbd = isb("qbd", [D, B, QG, H])
            ones = isb("ones", [1, 128], bf16)
            nmax, total = isb("nmax", [128, B]), isb("total", [128, B])
            p = isb("p", [128, B, T])
            pT = isb("pT", [128, 2, QT, 128])
            picked = isb("picked", [D, 2, QG, H])
            (ones_set, qbd_ready, scored, maxed, exped, inverted, averaged, turned, pT_ready, valued, masked,
             reg_done) = (sem(n) for n in ("ones_set", "qbd_ready", "scored", "maxed", "exped", "inverted",
                                           "averaged", "turned", "pT_ready", "valued", "masked", "reg_done"))
            with nc.Block() as block:
                @block.gpsimd
                def _(pool):
                    nc.gpsimd.memset(ones[:, :], 1.0).then_inc(ones_set, 1)
                    for b in range(B):
                        nc.gpsimd.tensor_tensor(qbd[:, b, :, :], q[:, b, 0:QG].unsqueeze(2).broadcast_to([D, QG, H]),
                                                g.c("headmask").unsqueeze(1).broadcast_to([D, QG, H]), ALU.mult)\
                            .then_inc(qbd_ready, 1)

                @block.tensor
                def _(pe):
                    pe.wait_ge(ones_set, 1)
                    for b in range(B):
                        pe.wait_ge(qbd_ready, b + 1)
                        nc.tensor.matmul(g.ps[:, b, :], qbd[:, b, :, :].rearrange("p c h -> p (c h)"), k[:, b, :],
                                         start=True, stop=False)
                        nc.tensor.matmul(g.ps[:, b, :], ones[:, :], lowered[:, b, :], start=False, stop=True)\
                            .then_inc(scored, 1)
                    for b in range(B):
                        pe.wait_ge(averaged, b + 1)
                        if b >= 2:
                            pe.wait_ge(pT_ready, b - 1)
                        for kt in range(QT):
                            last = nc.tensor.transpose(g.ps[:, 4 + b % 2, bass.ts(kt, 128)],
                                                       p[:, b, bass.ts(kt, 128)], g.c("ident"))
                        last.then_inc(turned, 1)
                        pe.wait_ge(pT_ready, b + 1)
                        if b >= 2:
                            pe.wait_ge(masked, b - 1)
                        for kt in range(QT):
                            last = nc.tensor.matmul(g.ps[:, 6 + b % 2, 0:128], v[:, QT * b + kt, :],
                                                    pT[:, b % 2, kt, :], start=kt == 0, stop=kt == QT - 1)
                        last.then_inc(valued, 1)

                @block.scalar
                def _(act):
                    for b in range(B):
                        act.wait_ge(maxed, b + 1)
                        nc.scalar.activation(p[:, b, :], g.ps[:, b, :], ACT.Exp, bias=nmax[:, b:b + 1], scale=SCALE,
                                             accum_out=total[:, b:b + 1]).then_inc(exped, 1)
                    for b in range(B):
                        act.wait_ge(turned, b + 1)
                        if b >= 2:
                            act.wait_ge(valued, b - 1)
                        nc.scalar.activation(pT[:, b % 2, :, :].rearrange("p t c -> p (t c)"), g.ps[:, 4 + b % 2, :],
                                             ACT.Identity).then_inc(pT_ready, 1)

                @block.vector
                def _(dve):
                    for b in range(B):
                        dve.wait_ge(scored, b + 1)
                        nc.vector.tensor_reduce(nmax[:, b:b + 1], g.ps[:, b, :], AX.X, ALU.max, negate=True)\
                            .then_inc(inverted, 1)
                        dve.wait_ge(inverted, b + 1)
                        nc.vector.tensor_single_scalar(nmax[:, b:b + 1], nmax[:, b:b + 1], SCALE, ALU.mult)\
                            .then_inc(maxed, 1)
                    for b in range(B):
                        dve.wait_ge(exped, b + 1)
                        nc.vector.reciprocal(total[:, b:b + 1], total[:, b:b + 1]).then_inc(inverted, 1)
                        dve.wait_ge(inverted, B + b + 1)
                        nc.vector.tensor_scalar(p[:, b, :], p[:, b, :], total[:, b:b + 1], None, ALU.mult)\
                            .then_inc(averaged, 1)
                    for b in range(B):
                        dve.wait_ge(valued, b + 1)
                        nc.vector.tensor_tensor(picked[:, b % 2, :, :],
                                                g.ps[:, 6 + b % 2, 0:128].rearrange("p (c h) -> p c h", h=H),
                                                g.c("headmask").unsqueeze(1).broadcast_to([D, QG, H]), ALU.mult)\
                            .then_inc(masked, 1)
                        dve.wait_ge(masked, b + 1)
                        nc.vector.tensor_reduce(reg_o[:, b, :], picked[:, b % 2, :, :], AX.X, ALU.add)\
                            .then_inc(reg_done, 1)

        def load(sp, qst, kst, b, at, loaded):
            for stack, first in ((qst, 0), (kst, 2)):
                src = rows_dram[first:first + 2, b, :].unsqueeze(1).broadcast_to([2, UH, T])
                sp.dma_start(stack[TERM_ROWS:TERM_ROWS + 2, at, :, :], src).then_inc(loaded, 16)
        w = g.w("gqkv")
        attention_stage(nc, g, "ga", xn, w[:, 0:D], w[:, D:2 * D], w[:, 2 * D:3 * D], 7, SCALE, o,
                        classes={"load": load, "loads": 2})
        halved, made, added = sem("halved"), sem("made"), sem("added")
        with nc.Block() as block:
            @block.vector
            def _(dve):
                nc.vector.tensor_tensor(o[:, :, 0:REG], o[:, :, 0:REG], reg_o[:, :, 0:REG], ALU.add)\
                    .then_inc(halved, 1)
                dve.wait_ge(halved, 1)
                nc.vector.tensor_single_scalar(o[:, :, 0:REG], o[:, :, 0:REG], 0.5, ALU.mult).then_inc(halved, 1)
                for b in range(B):
                    dve.wait_ge(made, b + 1)
                    nc.vector.scalar_tensor_tensor(out=g.x[:, bass.ts(b, T)], in0=g.ps[:, b, :],
                                                   scalar=g.v("b_proj"), in1=g.x[:, bass.ts(b, T)],
                                                   op0=ALU.add, op1=ALU.add).then_inc(added, 1)

            @block.tensor
            def _(pe):
                pe.wait_ge(halved, 2)
                for b in range(B):
                    nc.tensor.matmul(g.ps[:, b, :], g.w("gproj"), o[:, b, :], start=True, stop=True)\
                        .then_inc(made, 1)


def bf_constants(nc, g):
    with nc.Block() as block:
        @block.vector
        def _(dve):
            dve.wait_ge(g.const_loaded, 16)
            for to, name in ((g.ident_bf, "ident"), (g.lowered_bf, "lowered"), (g.loweredT_bf, "loweredT")):
                nc.vector.tensor_copy(to[:, :], g.c(name)).then_inc(g.cast, 1)



def store_stage(nc, g, out):
    with nc.Block() as block:
        @block.sync
        def _(sp):
            sp.wait_ge(g.x_loaded, 16)
            sp.wait_ge(g.const_loaded, 16)
            sp.wait_ge(g.vec_loaded, 16)
            for n in range(len(WEIGHT_GROUPS)):
                sp.wait_ge(g.weights_loaded[n], 16)
            sp.wait_ge(g.ctx_loaded, 32)
            sp.dma_start(out, g.x[:, :]).then_inc(g.stored, 16)
            sp.wait_ge(g.stored, 16)


def decoder_kernel(nc, ins, out):
    with ExitStack() as ctx:
        def sb(name, shape, dt=fp32):
            return ctx.enter_context(nc.sbuf_tensor(name, shape, dt))

        def sem(name):
            return ctx.enter_context(nc.semaphore(name))
        g = Core()
        g.x = sb("x", [D, NT])
        g.const = sb("const", [D, CONST_WIDTH])
        g.vec = sb("vec", [D, len(VECTORS)])
        g.eps = sb("eps", [D, 1])
        g.weights = sb("weights", [D, LAYER_WIDTH])
        g.ctxT = sb("ctxT", [D, B * LC])
        g.ctx = sb("ctx", [LC, B, D])
        g.ident_bf, g.lowered_bf, g.loweredT_bf = (sb(n, [D, D], bf16) for n in ("identb", "loweredb", "loweredTb"))
        g.ps = ctx.enter_context(nc.psum_tensor("ps", [D, 8, 512], fp32))
        g.x_loaded, g.const_loaded, g.vec_loaded, g.ctx_loaded = (
            sem(n) for n in ("x_loaded", "const_loaded", "vec_loaded", "ctx_loaded"))
        g.stored, g.cast = sem("stored"), sem("cast")
        g.weights_loaded = [sem(f"weights_loaded_{n}") for n in range(len(WEIGHT_GROUPS))]
        g.c = lambda n: g.const[:, CONST_COLS[n][0]:sum(CONST_COLS[n])]
        g.w = lambda n: g.weights[:, WEIGHT_COLS[n][0]:sum(WEIGHT_COLS[n])]
        g.v = lambda n: g.vec[:, VEC[n]:VEC[n] + 1]
        g.ones_dram, g.zeros_dram = ins["ones"], ins["zeros"]
        load_stage(nc, g, ins)
        rwkv_stage(nc, g)
        xattn_stage(nc, g)
        bf_constants(nc, g)
        ffn_stage(nc, g)
        load_layer_1(nc, g, ins)
        relative_stage(nc, g, ins)
        latent_stage(nc, g)
        grouped_stage(nc, g)
        store_stage(nc, g, out)


def kernel(**inputs):
    import numpy as _np
    import concourse.bacc as _bacc
    from concourse import mybir as _mybir
    from concourse.bass_utils import run_bass_kernel_spmd as _run

    i = {n: _np.asarray(a) for n, a in inputs.items()}

    def rows(a, n=128):
        return a.reshape(-1, n, a.shape[-1]).transpose(1, 0, 2).reshape(n, -1)

    def edges(a, before, after):
        return _np.concatenate([_np.repeat(a[:1], before, axis=0), a, _np.repeat(a[-1:], after, axis=0)])

    wvT = i["L0_attn_W_v"].T
    lo = i["L1_xattn_Wo"]
    weights = _np.concatenate([
        i["L0_attn_W_r"].T, i["L0_attn_W_k"].T, i["L0_attn_W_w"].T, wvT,
        _np.repeat(wvT.reshape(D, H, HD).transpose(0, 2, 1), HD, axis=2).reshape(D, HD * D),
        i["L0_attn_W_o"].T, i["L0_xattn_Wq"].T, i["L0_xattn_Wk"].T,
        i["L0_ffn_wq"], i["L0_ffn_wk"], i["L0_ffn_wv"], i["L0_ffn_wo"],
        i["L0_ffn_w1"], i["L0_ffn_w3"], rows(i["L0_ffn_w2"]),
        i["L0_ffn_router_w"],
        i["L0_ffn_ew1"].transpose(1, 0, 2).reshape(D, -1), i["L0_ffn_ew3"].transpose(1, 0, 2).reshape(D, -1),
        i["L0_ffn_ew2"].transpose(1, 0, 2).reshape(EH, -1),
        i["L1_attn_W_qkv"], i["L1_attn_W_out"],
        rows(i["L1_xattn_Wq"].T), i["L1_xattn_Wkv"], rows(lo),
        i["L1_ffn_W_qkv"], i["L1_ffn_W_proj"]], axis=1)
    b_qkv = i["L1_attn_b_qkv"]
    vec = _np.stack([
        i["L0_attn_tm_r"], i["L0_attn_tm_k"], i["L0_attn_tm_v"], i["L0_attn_tm_w"],
        i["L0_attn_u"].reshape(-1), _np.tile(i["L0_attn_ln_w"], H), _np.tile(i["L0_attn_ln_b"], H),
        i["L0_xattn_bq"], i["L0_xattn_bk"],
        i["L0_ffn_attn_norm_w"], i["L0_ffn_ff_norm_w"], i["L0_ffn_moe_norm_w"],
        b_qkv[0:D], b_qkv[D:2 * D], b_qkv[2 * D:], i["L1_attn_b_out"],
        i["L1_xattn_ln_l_w"], i["L1_xattn_ln_l_b"], i["L1_xattn_ln_c_w"], i["L1_xattn_ln_c_b"],
        i["L1_xattn_bo"], i["L1_ffn_g_info"].reshape(-1)[0:D], i["L1_ffn_b_proj"],
        _np.tile(i["L1_attn_rel_emb_k"][0], H), _np.tile(i["L1_attn_rel_emb_k"][-1], H)], axis=1)
    const = _np.concatenate(list(shape_constants().values()), axis=1).astype(_np.float32)
    arrays = {
        "xT": i["x"].reshape(NT, D).T,
        "ctxT": i["ctx_1024"].reshape(B * LC, D).T,
        "ctx": i["ctx_1024"].transpose(1, 0, 2),
        "ones": _np.ones((3, UH, T), "bfloat16"),
        "zeros": _np.zeros((3, UH, T), "bfloat16"),
        "rel_k": edges(i["L1_attn_rel_emb_k"], T + 7 - REL, T - 1 - REL).T,
        "rel_v": edges(i["L1_attn_rel_emb_v"], T - 1 - REL, T - 1 - REL),
        "weights": weights, "vec": vec, "const": const,
    }
    nc = _bacc.Bacc("TRN2", target_bir_lowering=False, num_devices=1)
    ins = {}
    for n, a in arrays.items():
        arrays[n] = _np.ascontiguousarray(a)
        ins[n] = nc.dram_tensor(f"in_{n}", arrays[n].shape, _mybir.dt.from_np(arrays[n].dtype),
                                kind="ExternalInput").ap()
    out = nc.dram_tensor("out_0", (D, NT), _mybir.dt.float32, kind="ExternalOutput").ap()
    decoder_kernel(nc, ins, out)
    r = _run(nc, [{f"in_{n}": a for n, a in arrays.items()}], core_ids=[0])
    return r.results[0]["out_0"].T.reshape(B, T, D)
```
